# Optimizing a Trainium2 kernel written in Bass

```python
import numpy as np
import jax
import jax.numpy as jnp

def _softmax(x, axis=-1):
    return jax.nn.softmax(x, axis=axis)

def _gelu(x):
    return jax.nn.gelu(x, approximate=True)

def _silu(x):
    return jax.nn.silu(x)

def _sigmoid(x):
    return jax.nn.sigmoid(x)

def _layernorm(x, axis=-1, eps=1e-05):
    m = jnp.mean(x, axis=axis, keepdims=True)
    v = jnp.var(x, axis=axis, keepdims=True)
    return (x - m) / jnp.sqrt(v + eps)

def _scatter_add(tgt, idx, src, axis=0):
    return tgt.at[idx].add(src)

def _segment_sum(src, seg, n):
    return jax.ops.segment_sum(src, seg, n)
kernel_name = 'mk_metaformer_d1_conv_nchw256_r4_4c8157'

def setup_inputs(seed: int=0):
    np.random.seed(seed)
    _w = jnp.asarray

    def _rec_inputs():
        import jax
        import jax.numpy as jnp
        _gk = jax.random.key(seed)
        x = -0.0003929 + 0.9999 * jax.random.normal(jax.random.fold_in(_gk, 1), (4, 64, 64, 16), jnp.float32)
        return x
    x = _rec_inputs()

    def _L0_conv_setup():
        import jax, jax.numpy as jnp
        import numpy as np
        from jax import lax

        def _dct_mat(N):
            n = np.arange(N)
            k = np.arange(N)[:, None]
            return jnp.asarray(2.0 * np.cos(np.pi * (2 * n + 1) * k / (2 * N)), jnp.float32)

        def _idct_mat(N):
            n = np.arange(N)[:, None]
            k = np.arange(N)
            w = np.ones(N)
            w[0] = 0.5
            return jnp.asarray(w * np.cos(np.pi * (2 * n + 1) * k / (2 * N)) / N, jnp.float32)

        def _l2norm(x, eps=1e-12):
            n = jnp.sqrt(jnp.sum(x * x, axis=-1, keepdims=True))
            return x / jnp.maximum(n, eps)
        key = jax.random.key(seed)
        ks = jax.random.split(key, 10)
        B, H, W, C = (4, 64, 64, 16)
        heads, dim_head = (4, 16)
        hd = heads * dim_head
        s = 0.05
        return {'x_input': jax.random.normal(ks[0], (B, H, W, C), jnp.float32), 'Wq': jax.random.normal(ks[1], (C, hd), jnp.float32) * s, 'Wk': jax.random.normal(ks[2], (C, hd), jnp.float32) * s, 'Wv': jax.random.normal(ks[3], (C, hd), jnp.float32) * s, 'rescale': jnp.ones((heads, 1, 1), jnp.float32), 'proj_w': jax.random.normal(ks[4], (hd, C), jnp.float32) * s, 'proj_b': jnp.zeros((C,), jnp.float32), 'c1a_w': jax.random.normal(ks[5], (C, C, 1, 1), jnp.float32) * s, 'c1b_w': jax.random.normal(ks[6], (C, 1, 3, 3), jnp.float32) * s, 'c2_w': jax.random.normal(ks[7], (C, C, 1, 1), jnp.float32) * s, 'coef_emb': jax.random.uniform(ks[8], (H, W), jnp.float32)}
    _L0_conv_all = _L0_conv_setup()
    _L0_conv_in = {k: v for k, v in _L0_conv_all.items() if k in ('Wq', 'Wk', 'Wv', 'rescale', 'proj_w', 'proj_b', 'c1a_w', 'c1b_w', 'c2_w', 'coef_emb')}
    del _L0_conv_all

    def _L0_ffn_setup():
        import jax, jax.numpy as jnp
        import numpy as np
        TOP_K = 2
        LN_EPS = 1e-05
        key = jax.random.key(seed)
        ks = jax.random.split(key, 8)
        B, S, D, E, H = (16, 256, 64, 8, 256)
        x = jax.random.normal(ks[0], (B, S, D), dtype=jnp.float32)
        Wr = jax.random.normal(ks[1], (D, E), dtype=jnp.float32) * 0.1
        br = jnp.zeros((E,), dtype=jnp.float32)
        ln_g = jnp.ones((E, D), dtype=jnp.float32)
        ln_b = jnp.zeros((E, D), dtype=jnp.float32)
        W1 = jax.random.normal(ks[2], (E, D, H), dtype=jnp.float32) * (1.0 / np.sqrt(D))
        b1 = jnp.zeros((E, H), dtype=jnp.float32)
        W2 = jax.random.normal(ks[3], (E, H, D), dtype=jnp.float32) * (1.0 / np.sqrt(H))
        b2 = jnp.zeros((E, D), dtype=jnp.float32)
        return {'x': x, 'Wr': Wr, 'br': br, 'ln_g': ln_g, 'ln_b': ln_b, 'W1': W1, 'b1': b1, 'W2': W2, 'b2': b2}
    _L0_ffn_all = _L0_ffn_setup()
    _L0_ffn_in = {k: v for k, v in _L0_ffn_all.items() if k in ('Wr', 'br', 'ln_g', 'ln_b', 'W1', 'b1', 'W2', 'b2')}
    del _L0_ffn_all
    return {'x': x, 'L0_conv_Wq': _L0_conv_in['Wq'], 'L0_conv_Wk': _L0_conv_in['Wk'], 'L0_conv_Wv': _L0_conv_in['Wv'], 'L0_conv_rescale': _L0_conv_in['rescale'], 'L0_conv_proj_w': _L0_conv_in['proj_w'], 'L0_conv_proj_b': _L0_conv_in['proj_b'], 'L0_conv_c1a_w': _L0_conv_in['c1a_w'], 'L0_conv_c1b_w': _L0_conv_in['c1b_w'], 'L0_conv_c2_w': _L0_conv_in['c2_w'], 'L0_conv_coef_emb': _L0_conv_in['coef_emb'], 'L0_ffn_Wr': _L0_ffn_in['Wr'], 'L0_ffn_br': _L0_ffn_in['br'], 'L0_ffn_ln_g': _L0_ffn_in['ln_g'], 'L0_ffn_ln_b': _L0_ffn_in['ln_b'], 'L0_ffn_W1': _L0_ffn_in['W1'], 'L0_ffn_b1': _L0_ffn_in['b1'], 'L0_ffn_W2': _L0_ffn_in['W2'], 'L0_ffn_b2': _L0_ffn_in['b2']}

def reference(x, L0_conv_Wq, L0_conv_Wk, L0_conv_Wv, L0_conv_rescale, L0_conv_proj_w, L0_conv_proj_b, L0_conv_c1a_w, L0_conv_c1b_w, L0_conv_c2_w, L0_conv_coef_emb, L0_ffn_Wr, L0_ffn_br, L0_ffn_ln_g, L0_ffn_ln_b, L0_ffn_W1, L0_ffn_b1, L0_ffn_W2, L0_ffn_b2):
    import jax
    import jax.numpy as jnp

    def _L0_conv_ref(x_input, Wq, Wk, Wv, rescale, proj_w, proj_b, c1a_w, c1b_w, c2_w, coef_emb):
        import jax, jax.numpy as jnp
        import numpy as np
        from jax import lax

        def _dct_mat(N):
            n = np.arange(N)
            k = np.arange(N)[:, None]
            return jnp.asarray(2.0 * np.cos(np.pi * (2 * n + 1) * k / (2 * N)), jnp.float32)

        def _idct_mat(N):
            n = np.arange(N)[:, None]
            k = np.arange(N)
            w = np.ones(N)
            w[0] = 0.5
            return jnp.asarray(w * np.cos(np.pi * (2 * n + 1) * k / (2 * N)) / N, jnp.float32)

        def _l2norm(x, eps=1e-12):
            n = jnp.sqrt(jnp.sum(x * x, axis=-1, keepdims=True))
            return x / jnp.maximum(n, eps)
        bs, H, W, C = x_input.shape
        K = 8
        hh, ww = (H // K, W // K)
        heads = rescale.shape[0]
        MH, MW = (_dct_mat(H), _dct_mat(W))
        x_in = jnp.transpose(x_input, (0, 3, 1, 2))
        x_dct = jnp.einsum('bchw,kw->bchk', x_in, MW)
        x_dct = jnp.einsum('bchw,kh->bckw', x_dct, MH)
        xb = x_dct.reshape(bs, C, hh, K, ww, K)
        x_tri = jnp.transpose(xb, (0, 2, 4, 3, 5, 1)).reshape(bs, hh * ww, K * K, C)

        def split(t):
            b, n, mm, hd = t.shape
            t = t.reshape(b, n, mm, heads, hd // heads)
            return jnp.transpose(t, (0, 1, 3, 4, 2))
        q = _l2norm(split(x_tri @ Wq))
        k = _l2norm(split(x_tri @ Wk))
        v = split(x_tri @ Wv)
        attn = jnp.einsum('bnhdm,bnhem->bnhde', q, k) * rescale[None, None]
        attn = jax.nn.softmax(attn, axis=-1)
        x0 = jnp.einsum('bnhde,bnhem->bnhdm', attn, v)
        x1 = jnp.transpose(x0, (0, 1, 4, 2, 3)).reshape(bs, hh * ww, K * K, -1)
        x2 = x1 @ proj_w + proj_b
        x3 = x2.reshape(bs, hh, ww, K, K, C)
        x_low = jnp.transpose(x3, (0, 5, 1, 3, 2, 4)).reshape(bs, C, H, W)
        dn = ('NCHW', 'OIHW', 'NCHW')
        g = lambda t: jax.nn.gelu(t, approximate=False)
        h1 = g(lax.conv_general_dilated(x_dct, c1a_w, (1, 1), 'VALID', dimension_numbers=dn))
        h1 = g(lax.conv_general_dilated(h1, c1b_w, (1, 1), ((1, 1), (1, 1)), dimension_numbers=dn, feature_group_count=C))
        x_conv = h1 + x_dct
        h2 = g(lax.conv_general_dilated(x_conv, c2_w, (1, 1), 'VALID', dimension_numbers=dn))
        x_high = h2 + x_conv
        coef = coef_emb[None, None]
        x_out = coef * x_low + (1.0 - coef) * x_high + x_dct
        IH, IW = (_idct_mat(H), _idct_mat(W))
        x_out = jnp.einsum('bchw,nw->bchn', x_out, IW)
        x_out = jnp.einsum('bchw,nh->bcnw', x_out, IH)
        return jnp.transpose(x_out, (0, 2, 3, 1))

    def _L0_ffn_ref(x, Wr, br, ln_g, ln_b, W1, b1, W2, b2):
        import jax, jax.numpy as jnp
        import numpy as np
        TOP_K = 2
        LN_EPS = 1e-05
        B, S, D = x.shape
        N = B * S
        xt = x.reshape(N, D)
        logits = xt @ Wr + br
        probs = jax.nn.softmax(logits, axis=-1)
        top_p, top_idx = jax.lax.top_k(probs, TOP_K)
        weights = top_p / top_p.sum(axis=-1, keepdims=True)
        mu = xt.mean(axis=-1, keepdims=True)
        var = ((xt - mu) ** 2).mean(axis=-1, keepdims=True)
        xn = (xt - mu) * jax.lax.rsqrt(var + LN_EPS)
        xe = xn[None, :, :] * ln_g[:, None, :] + ln_b[:, None, :]
        h = jax.nn.gelu(jnp.einsum('end,edh->enh', xe, W1) + b1[:, None, :], approximate=False)
        y = jnp.einsum('enh,ehd->end', h, W2) + b2[:, None, :]
        y_tok = jnp.transpose(y, (1, 0, 2))
        sel = jnp.take_along_axis(y_tok, top_idx[:, :, None], axis=1)
        out = (weights[:, :, None] * sel).sum(axis=1)
        return out.reshape(B, S, D)

    def _gn(v, G=32, eps=1e-05):
        B_, C_, H_, W_ = v.shape
        g = v.reshape(B_, G, C_ // G, H_, W_)
        m = jnp.mean(g, axis=(2, 3, 4), keepdims=True)
        s = jnp.var(g, axis=(2, 3, 4), keepdims=True)
        return ((g - m) / jnp.sqrt(s + eps)).reshape(v.shape)

    def _ln_c(v, eps=1e-06):
        m = jnp.mean(v, axis=1, keepdims=True)
        s = jnp.var(v, axis=1, keepdims=True)
        return (v - m) / jnp.sqrt(s + eps)

    def _ln_t(v, eps=1e-05):
        m = jnp.mean(v, axis=-1, keepdims=True)
        s = jnp.var(v, axis=-1, keepdims=True)
        return (v - m) / jnp.sqrt(s + eps)

    def _to_tokens(v):
        B_, C_, H_, W_ = v.shape
        return v.reshape(B_, C_, H_ * W_).transpose(0, 2, 1)

    def _from_tokens(t, like):
        B_, C_, H_, W_ = like.shape
        return t.transpose(0, 2, 1).reshape(B_, C_, H_, W_)
    x = x + _L0_conv_ref(_ln_c(x), L0_conv_Wq, L0_conv_Wk, L0_conv_Wv, L0_conv_rescale, L0_conv_proj_w, L0_conv_proj_b, L0_conv_c1a_w, L0_conv_c1b_w, L0_conv_c2_w, L0_conv_coef_emb)
    t = _to_tokens(x)
    t = t + _L0_ffn_ref(_ln_t(t), L0_ffn_Wr, L0_ffn_br, L0_ffn_ln_g, L0_ffn_ln_b, L0_ffn_W1, L0_ffn_b1, L0_ffn_W2, L0_ffn_b2)
    x = _from_tokens(t, x)
    return x

_drawn_inputs = setup_inputs


def setup_inputs(seed=0):
    import zlib

    import numpy as np

    out = dict(_drawn_inputs(seed))
    spreads = {'L0_conv_rescale': (1.0, 0.6),
     'L0_conv_proj_b': (0.0, 0.8),
     'L0_ffn_br': (0.0, 0.1),
     'L0_ffn_ln_g': (1.0, 0.2),
     'L0_ffn_ln_b': (0.0, 0.431),
     'L0_ffn_b1': (0.0, 0.41),
     'L0_ffn_b2': (0.0, 0.286)}
    factors = {'L0_conv_Wq': 8.0,
     'L0_conv_Wk': 8.0,
     'L0_conv_Wv': 5.998,
     'L0_conv_proj_w': 5.038,
     'L0_conv_c1a_w': 8.0,
     'L0_conv_c1b_w': 8.0}
    for name, (base, spread) in spreads.items():
        noise = np.random.default_rng([zlib.crc32(name.encode()), seed]).standard_normal(out[name].shape)
        drawn = base * np.exp(spread * noise) if base else spread * noise
        out[name] = jnp.asarray(drawn.astype(out[name].dtype))
    for name, factor in factors.items():
        out[name] = (out[name] * factor).astype(out[name].dtype)
    return out
```

```python
from contextlib import ExitStack

import numpy as np

import concourse.bass as bass
from concourse import mybir

P = 128
PAIRS, B2, H, W, C = 2, 2, 64, 64, 16
K = 8
WW = W // K
G = B2 * (H // K)
HEADS, DH = 4, 16
HD = HEADS * DH
E, HID = 8, 256
KT = HID // P
NT = E * KT
CP = C // 2
N = W * C
TT = N // P
CHUNK = 512
STEPS = PAIRS * N // CHUNK
LN1_EPS, LN_EPS, NORM_EPS = 1e-6, 1e-5, 1e-12

F32 = mybir.dt.float32
F16 = mybir.dt.float16
I32 = mybir.dt.int32
ALU = mybir.AluOpType
ACT = mybir.ActivationFunctionType
X = mybir.AxisListType.X

CONST = {}
at = 0
for name, n in (("dct_h", P), ("dct_w", P), ("idct_h", P), ("idct_w", P), ("ident", P), ("fold", H),
                ("shifted", (WW + 2) * C), ("diagonal", DH), ("small_index", E)):
    CONST[name] = slice(at, at + n)
    at += n
CONST_N = at


def constants():
    def twice(a):
        return np.kron(np.eye(2), a)
    n = np.arange(H)
    angle = np.cos(np.pi * (2 * n[None, :] + 1) * n[:, None] / (2 * H))
    dct = 2.0 * angle
    weight = np.ones(H)
    weight[0] = 0.5
    idct = (weight[:, None] * angle / H).T
    centred = dct - dct.mean(axis=1, keepdims=True)
    centred[1:] = dct[1:]
    centred[0] = 0.0
    block = np.zeros((P, (WW + 2) * C))
    for p in range(P):
        block[p, (p // C + 1) * C:(p // C + 2) * C] = 1
    out = np.zeros((P, CONST_N), np.float32)
    out[:, CONST["dct_h"]] = twice(centred.T)
    out[:, CONST["dct_w"]] = twice(dct.T)
    out[:, CONST["idct_h"]] = twice(idct.T)
    out[:, CONST["idct_w"]] = twice(idct.T)
    out[:, CONST["ident"]] = np.eye(P)
    out[:, CONST["fold"]] = np.tile(np.eye(H), (2, 1))
    out[:, CONST["shifted"]] = block
    out[:, CONST["diagonal"]] = np.tile(np.eye(DH), (P // DH, 1))
    out[:, CONST["small_index"]] = np.arange(E, 0, -1)[None, :]
    half = np.zeros((P, P + E // 2 * P), np.float16)
    half[:, :P] = np.eye(P)
    for r in range(2 * E):
        e = r % E
        half[r, P + (e // 2) * P + (e % 2) * H:P + (e // 2) * P + (e % 2) * H + H] = 1
    return out, half


SMALL = {}
at = 0
for name, n in (("wqk", 2 * HD), ("proj", HEADS * C), ("c1a", C), ("c2", C), ("wv_t", 2 * C), ("taps", 9), ("proj_b", 1),
                ("rescale", HEADS), ("ln_g", E), ("ln_b", E), ("b1", NT), ("b2", E // 2), ("wr", E), ("br", E),
                ("coef", H * K)):
    SMALL[name] = slice(at, at + n)
    at += n
SMALL_N = at


def small_weights(a):
    out = np.empty((P, SMALL_N), np.float32)

    def put(name, v):
        v = v.reshape(v.shape[0], -1)
        out[:, SMALL[name]] = np.tile(v, (P // v.shape[0], 1))
    put("wqk", np.concatenate([a["L0_conv_Wq"], a["L0_conv_Wk"]], axis=1))
    put("proj", a["L0_conv_proj_w"].reshape(HEADS, DH, C).transpose(1, 0, 2))
    put("c1a", a["L0_conv_c1a_w"].reshape(C, C).T)
    put("c2", a["L0_conv_c2_w"].reshape(C, C).T)
    wv = np.zeros((2, HD, 2, C), np.float32)
    for odd in range(2):
        wv[odd, :, odd] = a["L0_conv_Wv"].T
    put("wv_t", wv.reshape(P, 2 * C))
    put("taps", a["L0_conv_c1b_w"].reshape(C, 9))
    put("proj_b", a["L0_conv_proj_b"].reshape(C, 1))
    put("rescale", a["L0_conv_rescale"].reshape(1, HEADS))
    put("ln_g", a["L0_ffn_ln_g"].T)
    put("ln_b", a["L0_ffn_ln_b"].T)
    put("b1", a["L0_ffn_b1"].reshape(NT, P).T)
    put("b2", a["L0_ffn_b2"].reshape(E // 2, 2 * H).T)
    put("wr", a["L0_ffn_Wr"])
    put("br", a["L0_ffn_br"].reshape(1, E))
    put("coef", np.repeat(a["L0_conv_coef_emb"].reshape(H, WW, K).transpose(1, 0, 2), C, axis=0))
    return out


def metaformer(nc, x, small, W1, W2, const32, const16, out):
    ctx = ExitStack()
    with ctx:
        def sb(name, shape, dt=F32):
            return ctx.enter_context(nc.sbuf_tensor(name, shape, dt))

        def sem(name):
            return ctx.enter_context(nc.semaphore(name))

        psum = ctx.enter_context(nc.psum_tensor("psum", [P, 4, N], F32))
        SLOT = [psum[:, i, :] for i in range(4)]
        SA, SB_, SC, SD = SLOT

        c32 = sb("c32", [P, CONST_N])
        c16 = sb("c16", [P, P + E // 2 * P], F16)

        def const(name):
            return c32[:, CONST[name]]
        dct_h, dct_w, idct_h, idct_w, ident = (const(n) for n in ("dct_h", "dct_w", "idct_h", "idct_w", "ident"))
        mask = c32[:, CONST["shifted"].start + C:CONST["shifted"].start + C + P]
        ident16 = c16[:, 0:P]
        gate_rows = [c16[0:2 * E, P + m * P:P + (m + 1) * P] for m in range(E // 2)]
        sm = sb("sm", [P, SMALL_N])

        def weight(name):
            return sm[:, SMALL[name]]
        wqk = weight("wqk").rearrange("p (a n) -> p a n", a=2)
        proj = weight("proj").rearrange("p (h c) -> p h c", h=HEADS)
        c1a, c2, wv_t, taps = weight("c1a"), weight("c2"), weight("wv_t"), weight("taps")
        lng, lnb, b1t, b2t = weight("ln_g"), weight("ln_b"), weight("b1"), weight("b2")
        coef = weight("coef")
        wq_bd = sb("wq_bd", [P, HEADS, P])
        proj_bd = sb("proj_bd", [P, HEADS, P])
        conv_bd = sb("conv_bd", [P, 4, P])
        wv_rep = sb("wv_rep", [P, 2, P])
        w1f = sb("w1f", [P, E, HID])
        w1s = sb("w1s", [P, 2, E, HID], F16)
        w2 = sb("w2", [P, NT, H])
        b1p = sb("b1p", [P, NT])
        wrs = sb("wrs", [P, 2 * E], F16)

        xs = sb("xs", [P, PAIRS, N])
        x1 = sb("x1", [P, PAIRS, N])
        squares = sb("squares", [P, N])
        st = sb("st", [P, 12, G])
        dh = sb("dh", [P, N])
        dw = sb("dw", [P, K, P])
        xd = sb("xd", [P, P, K])
        xt = sb("xt", [P, N])
        gram = sb("gram", [P, G, P])
        tk = sb("tk", [P, HEADS, G, DH])
        prod = sb("prod", [P, G, 2, HD])
        inv_k = sb("inv_k", [P, G, HD])
        nq = sb("nq", [P, G * HEADS, DH])
        inv_q = sb("inv_q", [P, 3, G, HEADS])
        logit = sb("logit", [P, HEADS, G, DH])
        attn = sb("attn", [P, HEADS, G, DH])
        row = sb("row", [P, 3, HEADS * G])
        y_sb = gram[:, 0:G // 2, :].rearrange("p (a g) (c n) -> p (a g c) n", a=1, n=HD).rearrange("p g (h e) -> p g h e", e=DH)
        y_t = gram[:, G // 2:G, :].rearrange("p g n -> p (g n)")
        mix = prod[:, :, :, :].rearrange("p g a n -> p g (a n)")
        h_pad = sb("h_pad", [P, B2, H + 2, K + 2])
        dconv = sb("dconv", [P, B2, H, K])
        x_conv = sb("x_conv", [P, N])
        h2 = sb("h2", [P, N])
        x_high = sb("x_high", [P, N])
        both = sb("both", [P, N])
        x_out = sb("x_out", [P, K, P])
        back = sb("back", [P, C, WW, K])
        half_back = sb("half_back", [P, N])
        xc = sb("xc", [P, TT, B2, H])
        parts = sb("parts", [P, TT, B2, 2, H], F16)
        tok = sb("tok", [P, PAIRS, 2, B2, TT // 2 * P], F16)
        lg = sb("lg", [P, 8, G, E])
        rs = sb("rs", [P, 6, G])
        gate_parts = sb("gate_parts", [P, G, 2, E], F16)
        gates = sb("gates", [2 * E, PAIRS, 2, B2, TT // 2 * P], F16)

        hid = sb("hid", [P, 4, KT * CHUNK])
        gate_b = sb("gate_b", [P, 2, CHUNK])
        term = sb("term", [P, CHUNK])
        acc = sb("acc", [P, 2, CHUNK])

        x_in, const_in, weights_in = sem("x_in"), sem("const_in"), sem("weights_in")
        ffn_in, out_done = sem("ffn_in"), sem("out_done")
        act_chain, dve_chain, pool_chain = sem("act_chain"), sem("dve_chain"), sem("pool_chain")
        pad_zero, bd_ready, w1_ready = sem("pad_zero"), sem("bd_ready"), sem("w1_ready")
        bias_t, bias_ready, wr_ready = sem("bias_t"), sem("bias_ready"), sem("wr_ready")
        names = ("dct_h_done dct_w_done xd_done c1a_done halo_done xt_done gram_done t_done nq_done nk_done "
                 "logit_done c2_done y_done yt_done mix_done low_done back_done ih_done iw_done tokens_done "
                 "tok_done router_done gates_done").split()
        (dct_h_done, dct_w_done, xd_done, c1a_done, halo_done, xt_done, gram_done, t_done, nq_done, nk_done,
         logit_done, c2_done, y_done, yt_done, mix_done, low_done, back_done, ih_done, iw_done, tokens_done,
         tok_done, router_done, gates_done) = (sem(n) for n in names)
        names = ("sq_ready dh_ready dw_ready xd_ready xt_ready gram_ready tk_ready prod_ready nq_clamped "
                 "nk_clamped nq_root nk_root logit_ready exp_ready attn_ready y_ready yt_ready mix_ready h1_ready "
                 "dconv_ready dconv_gelu xconv_ready h2_ready both_ready xout_ready back_ready half_ready "
                 "x1_ready centred csq_ready xn_ready high_ready parts_ready tok_ready gap_ready tanh_ready "
                 "gparts_ready gates_ready low_read sums_read router_read").split()
        (sq_ready, dh_ready, dw_ready, xd_ready, xt_ready, gram_ready, tk_ready, prod_ready, nq_clamped,
         nk_clamped, nq_root, nk_root, logit_ready, exp_ready, attn_ready, y_ready, yt_ready, mix_ready, h1_ready,
         dconv_ready, dconv_gelu, xconv_ready, h2_ready, both_ready, xout_ready, back_ready, half_ready,
         x1_ready, centred, csq_ready, xn_ready, high_ready, parts_ready, tok_ready, gap_ready, tanh_ready,
         gparts_ready, gates_ready, low_read, sums_read, router_read) = (sem(n) for n in names)
        w1_done, gelu_ready, w2_done, gb_done, gb_ready, term_done, acc_ready, fold_done, res_ready, add_done = (
            sem(n) for n in ("w1_done gelu_ready w2_done gb_done gb_ready term_done acc_ready fold_done "
                             "res_ready add_done").split())

        block = ctx.enter_context(nc.Block())

        @block.sync
        def _(sp):
            for p in range(PAIRS):
                sp.dma_start(xs[:, p, :], x[B2 * p:B2 * p + B2].rearrange("b h c w -> (b h) (c w)")).then_inc(x_in, 16)
                if p == 0:
                    sp.dma_start(c32[:, :], const32).then_inc(const_in, 16)
            sp.dma_start(sm[:, :], small).then_inc(weights_in, 16)
            sp.dma_start(c16[:, :], const16).then_inc(const_in, 16)
            w1v = W1.rearrange("e d n -> d e n")
            for half in range(2):
                sp.dma_start(w1f[half * H:(half + 1) * H], w1v).then_inc(ffn_in, 16)
            sp.dma_start(w2[:, :, :], W2.rearrange("e (k p) d -> p (e k) d", p=P)).then_inc(ffn_in, 16)
            for i in range(STEPS):
                sp.wait_ge(res_ready, i + 1)
                pair, part = divmod(i, 2)
                view = out[B2 * pair:B2 * pair + B2].rearrange("b h c w -> (b h) (c w)")
                sp.dma_start(view[:, part * CHUNK:(part + 1) * CHUNK], x1[:, pair, part * CHUNK:(part + 1) * CHUNK]).then_inc(out_done, 16)
            sp.wait_ge(out_done, 16 * STEPS)

        @block.tensor
        def _(pe):
            def conv_half(p):
                pe.wait_ge(x_in, 16 * (p + 1))
                if p == 0:
                    pe.wait_ge(const_in, 32)
                else:
                    pe.wait_ge(router_read, p)
                for cp in range(CP):
                    mm = pe.matmul(SA[:, cp * P:(cp + 1) * P], xs[:, p, cp * P:(cp + 1) * P], dct_h, start=True, stop=True)
                mm.then_inc(dct_h_done, 1)
                pe.wait_ge(dh_ready, p + 1)
                if p:
                    pe.wait_ge(gates_ready, p)
                for cp in range(CP):
                    mm = pe.matmul(SB_[:, cp * P:(cp + 1) * P], dh[:, cp * P:(cp + 1) * P], dct_w, start=True, stop=True)
                mm.then_inc(dct_w_done, 1)
                pe.wait_ge(dw_ready, p + 1)
                if p:
                    pe.wait_ge(xn_ready, p)
                for k2 in range(K):
                    mm = pe.transpose(SC[:, k2 * P:(k2 + 1) * P], dw[:, k2, :], ident)
                mm.then_inc(xd_done, 1)
                pe.wait_ge(xd_ready, p + 1)
                if p == 0:
                    pe.wait_ge(bd_ready, 1)
                else:
                    pe.wait_ge(tok_ready, p)
                xf = xd[:, :, :].rearrange("p n k -> p (n k)")
                for j in range(2):
                    mm = pe.matmul(SD[:, j * CHUNK:(j + 1) * CHUNK], conv_bd[:, 0, :], xf[:, j * CHUNK:(j + 1) * CHUNK],
                                   start=True, stop=True)
                mm.then_inc(c1a_done, 1)
                pe.wait_ge(dh_ready, p + 1)
                pe.matmul(SA[:, 0:P], conv_bd[:, 1, :], xd[:, :, K - 1], start=True, stop=True)
                pe.matmul(SA[:, CHUNK:CHUNK + P], conv_bd[:, 2, :], xd[:, :, 0], start=True, stop=True).then_inc(halo_done, 1)
                pe.wait_ge(dw_ready, p + 1)
                for q in range(K):
                    mm = pe.transpose(SB_[:, q * P:(q + 1) * P], xf[:, q * P:(q + 1) * P], ident)
                mm.then_inc(xt_done, 1)
                pe.wait_ge(xt_ready, p + 1)
                pe.wait_ge(h1_ready, 2 * p + 1)
                for q in range(K):
                    for odd in range(2):
                        v = xt[odd * H:(odd + 1) * H, q * P:(q + 1) * P]
                        mm = pe.matmul(SLOT[2 + odd][:, q * P:(q + 1) * P], v, v, start=True, stop=True)
                mm.then_inc(gram_done, 1)
                pe.wait_ge(gram_ready, 2 * (p + 1))
                pe.wait_ge(h1_ready, 2 * (p + 1))
                if p == 0:
                    pe.wait_ge(weights_in, 16)
                wqk_all = wqk[:, :, :].rearrange("p a n -> p (a n)")
                for g in range(G):
                    mm = pe.matmul(SLOT[g // K][:, g % K * P:(g % K + 1) * P], gram[:, g, :], wqk_all, start=True, stop=True)
                mm.then_inc(t_done, 1)
                pe.wait_ge(prod_ready, 2 * (p + 1))
                for a, done, slot in ((0, nq_done, SC), (1, nk_done, SD)):
                    for j in range(2):
                        mm = pe.matmul(slot[:, j * CHUNK:(j + 1) * CHUNK], mask, prod[:, j * K:(j + 1) * K, a, :],
                                       start=True, stop=True)
                    mm.then_inc(done, 1)
                pe.wait_ge(tk_ready, 2 * (p + 1))
                for h in range(HEADS):
                    mm = pe.matmul(SA[:, h * G * DH:(h + 1) * G * DH], wq_bd[:, h, :],
                                   tk[:, h, :, :].rearrange("p g e -> p (g e)"), start=True, stop=True)
                mm.then_inc(logit_done, 1)
                pe.wait_ge(xconv_ready, p + 1)
                for j in range(2):
                    mm = pe.matmul(SB_[:, j * CHUNK:(j + 1) * CHUNK], conv_bd[:, 3, :], x_conv[:, j * CHUNK:(j + 1) * CHUNK],
                                   start=True, stop=True)
                mm.then_inc(c2_done, 1)
                pe.wait_ge(attn_ready, p + 1)
                for h in range(HEADS):
                    mm = pe.matmul(SC[:, h * G * DH:(h + 1) * G * DH], proj_bd[:, h, :],
                                   attn[:, h, :, :].rearrange("p g e -> p (g e)"), start=True, stop=True)
                mm.then_inc(y_done, 1)
                pe.wait_ge(y_ready, p + 1)
                pe.wait_ge(nk_clamped, p + 1)
                for q in range(K):
                    mm = pe.transpose(SD[:, q * P:(q + 1) * P],
                                      y_sb[:, 2 * q:2 * q + 2, :, :].rearrange("p g h e -> p (g h e)"), ident)
                mm.then_inc(yt_done, 1)
                pe.wait_ge(yt_ready, p + 1)
                pe.wait_ge(logit_ready, p + 1)
                pe.wait_ge(h2_ready, p + 1)
                for odd in range(2):
                    for j in range(2):
                        mm = pe.matmul(SLOT[odd][:, j * CHUNK:(j + 1) * CHUNK], wv_rep[:, odd, :],
                                       y_t[:, j * CHUNK:(j + 1) * CHUNK], start=True, stop=True)
                mm.then_inc(mix_done, 1)
                pe.wait_ge(mix_ready, 2 * (p + 1))
                for g in range(G):
                    mm = pe.matmul(SC[:, g * H:(g + 1) * H], mix[:, g, :], xf[:, g * H:(g + 1) * H], start=True, stop=True)
                mm.then_inc(low_done, 1)
                pe.wait_ge(xout_ready, p + 1)
                for k2 in range(K):
                    mm = pe.transpose(SD[:, k2 * P:(k2 + 1) * P], x_out[:, k2, :], ident)
                mm.then_inc(back_done, 1)
                pe.wait_ge(back_ready, p + 1)
                bf = back[:, :, :, :].rearrange("p c w k -> p (c w k)")
                for cp in range(CP):
                    mm = pe.matmul(SA[:, cp * P:(cp + 1) * P], bf[:, cp * P:(cp + 1) * P], idct_h, start=True, stop=True)
                mm.then_inc(ih_done, 1)
                pe.wait_ge(half_ready, p + 1)
                for cp in range(CP):
                    mm = pe.matmul(SB_[:, cp * P:(cp + 1) * P], half_back[:, cp * P:(cp + 1) * P], idct_w, start=True, stop=True)
                mm.then_inc(iw_done, 1)
                pe.wait_ge(x1_ready, p + 1)
                for j in range(TT):
                    mm = pe.transpose(SC[:, j * P:(j + 1) * P], x1[:, p, j * P:(j + 1) * P], ident)
                mm.then_inc(tokens_done, 1)
                pe.wait_ge(parts_ready, p + 1)
                sd16 = SD.bitcast(F16)
                for j in range(TT):
                    for b in range(B2):
                        a = (j // 4 * 2 + b) * CHUNK + j % 4 * P
                        mm = pe.transpose(sd16[:, a:a + P], parts[:, j, b, :, :].rearrange("p a h -> p (a h)"), ident16)
                mm.then_inc(tok_done, 1)
                pe.wait_ge(tok_ready, p + 1)
                if p == 0:
                    pe.wait_ge(wr_ready, 1)
                for j in range(TT):
                    for b in range(B2):
                        t = j * B2 + b
                        mm = pe.matmul(SA[:, t * 2 * E:(t + 1) * 2 * E],
                                       tok[:, p, j // 4, b, j % 4 * P:(j % 4 + 1) * P], wrs[:, :], start=True, stop=True)
                mm.then_inc(router_done, 1)
                pe.wait_ge(gparts_ready, p + 1)
                sb16 = SB_.bitcast(F16)
                for j in range(TT):
                    for b in range(B2):
                        a = (j // 4 * 2 + b) * CHUNK + j % 4 * P
                        mm = pe.transpose(sb16[0:2 * E, a:a + P],
                                          gate_parts[:, j * B2 + b, :, :].rearrange("p a e -> p (a e)"), ident16)
                mm.then_inc(gates_done, 1)

            pe.wait_ge(weights_in, 16)
            pe.wait_ge(ffn_in, 16 * 3)
            for t in range(NT):
                mm = pe.matmul(SD[:, t:t + 1], w1f[0:H, t // KT, t % KT * P:(t % KT + 1) * P], lnb[0:H, t // KT:t // KT + 1],
                               start=True, stop=True)
            mm.then_inc(bias_t, 1)
            pe.wait_ge(bias_ready, 1)
            for p in range(PAIRS):
                conv_half(p)

            hbank = [SA, SB_]
            ybank = [SC[:, 0:CHUNK], SC[:, CHUNK:N]]
            gbank, fbank = SD[:, 0:CHUNK], SD[:, CHUNK:N]
            tokf = tok[:, :, :, :, :].rearrange("p a j b n -> p (a j b n)")
            gatef = gates[:, :, :, :, :].rearrange("p a j b n -> p (a j b n)")

            def up(i, b, e, first):
                if not (first and b == 0 and e < 2):
                    pe.wait_ge(gelu_ready, (2 * i + b) * E + e - 1)
                for k in range(KT):
                    for part in range(2):
                        mm = pe.matmul(hbank[e % 2][:, k * CHUNK:(k + 1) * CHUNK], w1s[:, part, e, k * P:(k + 1) * P],
                                       tokf[:, bass.ds((2 * i + b) * CHUNK, CHUNK)], start=part == 0, stop=part == 1)
                mm.then_inc(w1_done, 1)

            def gate(i, b, m):
                pe.matmul(gbank, gate_rows[m], gatef[:, bass.ds((2 * i + b) * CHUNK, CHUNK)], start=True,
                          stop=True).then_inc(gb_done, 1)

            def down(i, b, m, first):
                pe.wait_ge(gb_ready, (2 * i + b) * 4 + m + 1)
                pe.wait_ge(gelu_ready, (2 * i + b) * E + 2 * m + 2)
                if not (first and b == 0 and m < 2):
                    pe.wait_ge(term_done, (2 * i + b) * 4 + m - 1)
                for k in range(KT):
                    for odd in range(2):
                        mm = pe.matmul(ybank[m % 2][odd * H:(odd + 1) * H, :], w2[:, (2 * m + odd) * KT + k, :],
                                       hid[:, (2 * m + odd) % 4, k * CHUNK:(k + 1) * CHUNK], start=k == 0, stop=k == KT - 1)
                mm.then_inc(w2_done, 1)

            def fold(i, b, first=False):
                pe.wait_ge(acc_ready, 2 * i + b + 1)
                if b == 0 and not first:
                    pe.wait_ge(res_ready, i)
                pe.matmul(fbank[b * H:(b + 1) * H, :], const("fold"), acc[:, b, :], start=True, stop=True).then_inc(fold_done, 1)

            def step(i, first):
                for b in range(B2):
                    up(i, b, 0, first)
                    up(i, b, 1, first)
                    if b == 1:
                        fold(i, 0, first)
                    elif not first:
                        fold(i - 1, 1)
                    for m in range(E // 2):
                        gate(i, b, m)
                        if m < E // 2 - 1:
                            up(i, b, 2 * m + 2, first)
                            up(i, b, 2 * m + 3, first)
                        down(i, b, m, first)

            pe.wait_ge(gates_ready, PAIRS)
            pe.wait_ge(w1_ready, 1)
            step(0, True)
            with pe.Fori(1, STEPS) as i:
                step(i, False)
            fold(STEPS - 1, 1)

        @block.scalar
        def _(act):
            links = [0]

            def link(ins):
                links[0] += 1
                ins.then_inc(act_chain, 1)
                act.wait_ge(act_chain, links[0])

            for p in range(PAIRS):
                act.wait_ge(dct_h_done, p + 1)
                act.activation(squares[:, :], SA, ACT.Square).then_inc(sq_ready, 1)
                act.wait_ge(dct_w_done, p + 1)
                act.copy(dw[:, :, :].rearrange("p k (w c) -> p c w k", c=C), SB_.rearrange("p (c w k) -> p c w k", c=C, k=K)).then_inc(dw_ready, 1)
                act.wait_ge(xd_done, p + 1)
                act.copy(xd[:, :, :].rearrange("p n k -> p k n"), SC.rearrange("p (k n) -> p k n", k=K)).then_inc(xd_ready, 1)
                if p == 0:
                    act.wait_ge(pad_zero, 1)
                else:
                    act.wait_ge(dconv_ready, p)
                act.wait_ge(c1a_done, p + 1)
                for b in range(B2):
                    g = act.activation(h_pad[:, b, 1:H + 1, 1:K + 1],
                                       SD[:, b * CHUNK:(b + 1) * CHUNK].rearrange("p (h k) -> p h k", k=K), ACT.Gelu)
                g.then_inc(h1_ready, 1)
                act.wait_ge(halo_done, p + 1)
                act.activation(h_pad[:, :, 1:H + 1, 0], SA[:, 0:P].rearrange("p (b h) -> p b h", b=B2), ACT.Gelu)
                act.activation(h_pad[:, :, 1:H + 1, K + 1], SA[:, CHUNK:CHUNK + P].rearrange("p (b h) -> p b h", b=B2),
                               ACT.Gelu).then_inc(h1_ready, 1)
                act.wait_ge(xt_done, p + 1)
                act.copy(xt[:, :], SB_).then_inc(xt_ready, 1)
                act.wait_ge(t_done, p + 1)
                for j in range(2):
                    act.wait_ge(prod_ready, 2 * p + j + 1)
                    act.copy(tk[:, :, j * K:(j + 1) * K, :].rearrange("p h g e -> p g h e"),
                             SLOT[j].rearrange("p (g a h e) -> p g a h e", a=2, h=HEADS, e=DH)[:, :, 1, :, :]).then_inc(tk_ready, 1)
                act.wait_ge(dconv_ready, p + 1)
                act.activation(x_conv[:, :], dconv[:, :, :, :].rearrange("p b h k -> p (b h k)"), ACT.Gelu).then_inc(dconv_gelu, 1)
                act.wait_ge(c2_done, p + 1)
                act.activation(h2[:, :], SB_, ACT.Gelu).then_inc(h2_ready, 1)
                act.wait_ge(nk_clamped, p + 1)
                act.activation(inv_k[:, :, :], inv_k[:, :, :], ACT.Sqrt).then_inc(nk_root, 1)
                act.wait_ge(nq_clamped, p + 1)
                act.activation(inv_q[:, 1, :, :], inv_q[:, 0, :, :], ACT.Sqrt).then_inc(nq_root, 1)
                act.wait_ge(logit_ready, p + 1)
                act.activation(attn[:, :, :, :], logit[:, :, :, :], ACT.Exp).then_inc(exp_ready, 1)
                act.wait_ge(y_done, p + 1)
                act.copy(y_sb[:, :, :, :].rearrange("p g h e -> p h g e"), SC.rearrange("p (h g e) -> p h g e", h=HEADS, g=G)).then_inc(y_ready, 1)
                act.wait_ge(yt_done, p + 1)
                act.copy(y_t[:, :], SD).then_inc(yt_ready, 1)
                act.wait_ge(back_done, p + 1)
                act.copy(back[:, :, :, :].rearrange("p c w k -> p k w c"), SD.rearrange("p (k w c) -> p k w c", k=K, c=C)).then_inc(back_ready, 1)
                act.wait_ge(ih_done, p + 1)
                act.copy(half_back[:, :], SA).then_inc(half_ready, 1)
                act.wait_ge(centred, p + 1)
                act.activation(squares[:, :], xc[:, :, :, :].rearrange("p j b h -> p (j b h)"), ACT.Square).then_inc(csq_ready, 1)
                act.wait_ge(xn_ready, p + 1)
                act.copy(parts[:, :, :, 0, :], xc[:, :, :, :]).then_inc(high_ready, 1)
                act.wait_ge(tok_done, p + 1)
                act.copy(tok[:, p, :, :, :].rearrange("p j b n -> p (j b n)"), SD.bitcast(F16)[:, 0:2 * N]).then_inc(tok_ready, 1)
                act.wait_ge(gap_ready, p + 1)
                act.activation(rs[:, 3, :], rs[:, 2, :], ACT.Tanh, scale=0.5).then_inc(tanh_ready, 1)
                act.wait_ge(gates_done, p + 1)
                act.copy(gates[:, p, :, :, :].rearrange("p j b n -> p (j b n)"), SB_.bitcast(F16)[0:2 * E, 0:2 * N]).then_inc(gates_ready, 1)

            hbank = [SA, SB_]
            gbank = SD[:, 0:CHUNK]

            def gelu(i, b, e, first):
                act.wait_ge(w1_done, (2 * i + b) * E + e + 1)
                if not (first and b == 0 and e < 4):
                    act.wait_ge(w2_done, (2 * i + b) * 4 + e // 2 - 1)
                for k in range(KT):
                    a = act.activation(hid[:, e % 4, k * CHUNK:(k + 1) * CHUNK], hbank[e % 2][:, k * CHUNK:(k + 1) * CHUNK],
                                       ACT.Gelu, bias=b1p[:, e * KT + k:e * KT + k + 1])
                a.then_inc(gelu_ready, 1)

            def spread(i, b, m, first):
                act.wait_ge(gb_done, (2 * i + b) * 4 + m + 1)
                if not (first and b == 0 and m < 2):
                    act.wait_ge(term_done, (2 * i + b) * 4 + m - 1)
                act.copy(gate_b[:, m % 2, :], gbank).then_inc(gb_ready, 1)

            def step(i, first):
                for b in range(B2):
                    gelu(i, b, 0, first)
                    gelu(i, b, 1, first)
                    for m in range(E // 2):
                        spread(i, b, m, first)
                        if m < E // 2 - 1:
                            gelu(i, b, 2 * m + 2, first)
                            gelu(i, b, 2 * m + 3, first)

            act.wait_ge(bias_ready, 1)
            step(0, True)
            with act.Fori(1, STEPS) as i:
                step(i, False)

        @block.gpsimd
        def _(pool):
            pool.memset(h_pad[:, :, :, :], 0.0).then_inc(pad_zero, 1)
            pool.wait_ge(const_in, 32)
            pool.wait_ge(weights_in, 16)
            shifted = const("shifted").rearrange("p (b c) -> p b c", c=C)

            def diagonal(dst, src, blocks):
                return pool.tensor_tensor(dst.rearrange("p (b c) -> p b c", c=C), shifted[:, blocks:blocks + WW, :],
                                          src.unsqueeze(1).broadcast_to([P, WW, C]), ALU.mult)

            diagonal(conv_bd[:, 0, :], c1a, 1)
            diagonal(conv_bd[:, 1, :], c1a, 0)
            diagonal(conv_bd[:, 2, :], c1a, 2)
            diagonal(conv_bd[:, 3, :], c2, 1)
            for h in range(HEADS):
                diagonal(wq_bd[:, h, :], wqk[:, 0, h * DH:(h + 1) * DH], 1)
                diagonal(proj_bd[:, h, :], proj[:, h, :], 1)
            for odd in range(2):
                last = pool.tensor_copy(wv_rep[:, odd, :].rearrange("p (b c) -> p b c", c=C),
                                        wv_t[:, odd * C:(odd + 1) * C].unsqueeze(1).broadcast_to([P, WW, C]))
            last.then_inc(bd_ready, 1)
            pool.wait_ge(ffn_in, 16 * 3)
            pool.wait_ge(bias_t, 1)
            pool.tensor_tensor(w1f[:, :, :], w1f[:, :, :], lng.unsqueeze(2).broadcast_to([P, E, HID]),
                               ALU.mult).then_inc(pool_chain, 1)
            pool.wait_ge(pool_chain, 1)
            pool.tensor_copy(w1s[:, 0, :, :], w1f[:, :, :]).then_inc(pool_chain, 1)
            pool.wait_ge(pool_chain, 2)
            pool.tensor_tensor(w1s[:, 1, :, :], w1f[:, :, :], w1s[:, 0, :, :], ALU.subtract).then_inc(w1_ready, 1)
            pool.tensor_copy(wrs[:, 0:E], weight("wr")).then_inc(pool_chain, 1)
            pool.wait_ge(pool_chain, 3)
            pool.tensor_tensor(wrs[:, E:2 * E], weight("wr"), wrs[:, 0:E], ALU.subtract).then_inc(wr_ready, 1)

        @block.vector
        def _(dve):
            links = [0]

            def link(ins):
                links[0] += 1
                ins.then_inc(dve_chain, 1)
                dve.wait_ge(dve_chain, links[0])

            def flat(t):
                return t.rearrange("p a b -> p (a b)")

            def inverse_root(dst, src, tmp, tmp2):
                link(dve.tensor_scalar(tmp.bitcast(I32), src.bitcast(I32), 1, None, ALU.logical_shift_right))
                link(dve.tensor_scalar(dst.bitcast(I32), tmp.bitcast(I32), -1.0, float(0x5F3759DF), ALU.mult, ALU.add))
                for _ in range(4):
                    link(dve.tensor_tensor(tmp, dst, dst, ALU.mult))
                    link(dve.tensor_tensor(tmp2, tmp, src, ALU.mult))
                    link(dve.tensor_scalar(tmp, tmp2, -0.5, 1.5, ALU.mult, ALU.add))
                    link(dve.tensor_tensor(dst, dst, tmp, ALU.mult))

            dve.wait_ge(weights_in, 16)
            dve.wait_ge(bias_t, 1)
            dve.tensor_tensor(b1p[:, :], SD[:, 0:NT], b1t, ALU.add).then_inc(bias_ready, 1)

            for p in range(PAIRS):
                dve.wait_ge(sq_ready, p + 1)
                link(dve.tensor_reduce(st[:, 0, :], squares[:, :].rearrange("p (g h) -> p g h", h=H), X, ALU.add))
                link(dve.tensor_scalar(st[:, 1, :], st[:, 0, :], 1.0 / (2 * H * H), LN1_EPS, ALU.mult, ALU.add))
                inverse_root(st[:, 2, :], st[:, 1, :], st[:, 3, :], st[:, 4, :])
                dve.tensor_tensor(dh[:, :].rearrange("p (g h) -> p g h", h=H), SA.rearrange("p (g h) -> p g h", h=H),
                                  st[:, 2, :].unsqueeze(2).broadcast_to([P, G, H]), ALU.mult).then_inc(dh_ready, 1)
                dve.wait_ge(gram_done, p + 1)
                gv = gram[:, :, :].rearrange("p (q o) n -> p q o n", o=2)
                for odd in range(2):
                    dve.tensor_tensor(gv[:, :, odd, :], SLOT[2 + odd].rearrange("p (q n) -> p q n", n=P),
                                      mask.unsqueeze(1).broadcast_to([P, K, P]), ALU.mult).then_inc(gram_ready, 1)
                dve.wait_ge(t_done, p + 1)
                for j in range(2):
                    dve.tensor_tensor(prod[:, j * K:(j + 1) * K, :, :].rearrange("p g a n -> p g (a n)"),
                                      SLOT[j].rearrange("p (g n) -> p g n", n=P),
                                      wqk[:, :, :].rearrange("p a n -> p (a n)").unsqueeze(1).broadcast_to([P, K, P]),
                                      ALU.mult).then_inc(prod_ready, 1)
                dve.wait_ge(h1_ready, 2 * (p + 1))
                if p:
                    dve.wait_ge(dconv_gelu, p)
                for tap in range(9):
                    y, xx = divmod(tap, 3)
                    for b in range(B2):
                        src = h_pad[:, b, y:y + H, xx:xx + K]
                        w = taps[:, tap:tap + 1]
                        if tap == 0:
                            last = dve.tensor_scalar(dconv[:, b, :, :], src, w, None, ALU.mult)
                        else:
                            last = dve.scalar_tensor_tensor(dconv[:, b, :, :], src, w, dconv[:, b, :, :], ALU.mult, ALU.add)
                        if tap < 8:
                            if b == 1:
                                link(last)
                            else:
                                last.then_inc(dve_chain, 1)
                                links[0] += 1
                last.then_inc(dconv_ready, 1)
                dve.wait_ge(nk_done, p + 1)
                dve.tensor_scalar(inv_k[:, :, :].rearrange("p g n -> p (g n)"), SD, NORM_EPS ** 2, None, ALU.max).then_inc(nk_clamped, 1)
                dve.wait_ge(nq_done, p + 1)
                link(dve.tensor_tensor(nq[:, :, :], SC.rearrange("p (g d) -> p g d", d=DH),
                                       const("diagonal").unsqueeze(1).broadcast_to([P, G * HEADS, DH]), ALU.mult))
                link(dve.tensor_reduce(inv_q[:, 1, :, :].rearrange("p g h -> p (g h)"), nq[:, :, :], X, ALU.add))
                dve.tensor_scalar(inv_q[:, 0, :, :], inv_q[:, 1, :, :], NORM_EPS ** 2, None, ALU.max).then_inc(nq_clamped, 1)
                dve.wait_ge(dconv_gelu, p + 1)
                dve.tensor_tensor(x_conv[:, :], x_conv[:, :], flat(xd[:, :, :]), ALU.add).then_inc(xconv_ready, 1)
                dve.wait_ge(nk_root, p + 1)
                link(dve.reciprocal(inv_k[:, :, :], inv_k[:, :, :]))
                dve.wait_ge(nq_root, p + 1)
                link(dve.reciprocal(inv_q[:, 2, :, :], inv_q[:, 1, :, :]))
                link(dve.tensor_tensor(inv_q[:, 0, :, :], inv_q[:, 2, :, :],
                                       weight("rescale").unsqueeze(1).broadcast_to([P, G, HEADS]), ALU.mult))
                dve.wait_ge(logit_done, p + 1)
                link(dve.tensor_tensor(logit[:, :, :, :], SA.rearrange("p (h g e) -> p h g e", h=HEADS, g=G),
                                       inv_k[:, :, :].rearrange("p g (h e) -> p h g e", h=HEADS), ALU.mult))
                lf = logit[:, :, :, :].rearrange("p h g e -> p (h g) e")
                link(dve.tensor_tensor(logit[:, :, :, :], logit[:, :, :, :],
                                       inv_q[:, 0, :, :].rearrange("p g h -> p h g").unsqueeze(3).broadcast_to([P, HEADS, G, DH]), ALU.mult))
                link(dve.tensor_reduce(row[:, 0, :], lf, X, ALU.max))
                dve.tensor_tensor(lf, lf, row[:, 0, :].unsqueeze(2).broadcast_to([P, HEADS * G, DH]),
                                  ALU.subtract).then_inc(logit_ready, 1)
                af = attn[:, :, :, :].rearrange("p h g e -> p (h g) e")
                dve.wait_ge(exp_ready, p + 1)
                link(dve.tensor_reduce(row[:, 1, :], af, X, ALU.add))
                link(dve.reciprocal(row[:, 2, :], row[:, 1, :]))
                dve.tensor_tensor(af, af, row[:, 2, :].unsqueeze(2).broadcast_to([P, HEADS * G, DH]),
                                  ALU.mult).then_inc(attn_ready, 1)
                dve.wait_ge(h2_ready, p + 1)
                link(dve.tensor_tensor(x_high[:, :], h2[:, :], x_conv[:, :], ALU.add))
                link(dve.tensor_tensor(both[:, :], x_high[:, :], flat(xd[:, :, :]), ALU.add))
                dve.wait_ge(mix_done, p + 1)
                mv = mix[:, :, :].rearrange("p (q o) n -> p q o n", o=2)
                for odd in range(2):
                    dve.tensor_tensor(mv[:, :, odd, :], SLOT[odd].rearrange("p (q n) -> p q n", n=P),
                                      mask.unsqueeze(1).broadcast_to([P, K, P]), ALU.mult).then_inc(mix_ready, 1)
                dve.wait_ge(low_done, p + 1)
                link(dve.scalar_tensor_tensor(h2[:, :], SC, weight("proj_b"), x_high[:, :], ALU.add, ALU.subtract))
                link(dve.tensor_tensor(h2[:, :].rearrange("p (b n) -> p b n", b=B2), h2[:, :].rearrange("p (b n) -> p b n", b=B2),
                                       coef.unsqueeze(1).broadcast_to([P, B2, CHUNK]), ALU.mult))
                dve.tensor_tensor(x_out[:, :, :], h2[:, :].rearrange("p (n k) -> p k n", k=K),
                                  both[:, :].rearrange("p (n k) -> p k n", k=K), ALU.add).then_inc(xout_ready, 1)
                dve.wait_ge(iw_done, p + 1)
                dve.tensor_tensor(x1[:, p, :], SB_, xs[:, p, :], ALU.add).then_inc(x1_ready, 1)
                dve.wait_ge(tokens_done, p + 1)
                tv = SC.rearrange("p (t h) -> p t h", h=H)
                xv = xc[:, :, :, :].rearrange("p j b h -> p (j b) h")
                link(dve.tensor_reduce(st[:, 5, :], tv, X, ALU.add))
                link(dve.tensor_scalar(st[:, 6, :], st[:, 5, :], 1.0 / H, None, ALU.mult))
                dve.tensor_tensor(xv, tv, st[:, 6, :].unsqueeze(2).broadcast_to([P, G, H]), ALU.subtract).then_inc(centred, 1)
                dve.wait_ge(csq_ready, p + 1)
                link(dve.tensor_reduce(st[:, 0, :], squares[:, :].rearrange("p (t h) -> p t h", h=H), X, ALU.add))
                link(dve.tensor_scalar(st[:, 1, :], st[:, 0, :], 1.0 / H, None, ALU.mult))
                link(dve.tensor_scalar(st[:, 2, :], st[:, 1, :], LN_EPS, None, ALU.add))
                inverse_root(st[:, 3, :], st[:, 2, :], st[:, 7, :], st[:, 8, :])
                link(dve.tensor_tensor(st[:, 4, :], st[:, 3, :], st[:, 3, :], ALU.mult))
                link(dve.tensor_tensor(st[:, 5, :], st[:, 4, :], st[:, 1, :], ALU.mult))
                link(dve.tensor_scalar(st[:, 6, :], st[:, 5, :], LN_EPS, None, ALU.add))
                inverse_root(st[:, 9, :], st[:, 6, :], st[:, 7, :], st[:, 8, :])
                link(dve.tensor_tensor(st[:, 4, :], st[:, 3, :], st[:, 9, :], ALU.mult))
                link(dve.tensor_tensor(st[:, 10, :], st[:, 6, :], st[:, 9, :], ALU.mult))
                dve.tensor_tensor(xv, xv, st[:, 4, :].unsqueeze(2).broadcast_to([P, G, H]), ALU.mult).then_inc(xn_ready, 1)
                dve.wait_ge(high_ready, p + 1)
                dve.tensor_tensor(parts[:, :, :, 1, :], xc[:, :, :, :], parts[:, :, :, 0, :], ALU.subtract).then_inc(parts_ready, 1)
                L = [lg[:, n, :, :] for n in range(8)]

                def wide(v):
                    return v.unsqueeze(2).broadcast_to([P, G, E])

                index = const("small_index").unsqueeze(1).broadcast_to([P, G, E])
                dve.wait_ge(router_done, p + 1)
                rv = SA[:, 0:G * 2 * E].rearrange("p (t a e) -> p t a e", a=2, e=E)
                link(dve.tensor_copy(L[0], rv[:, :, 0, :]))
                dve.tensor_tensor(L[1], L[0], rv[:, :, 1, :], ALU.add).then_inc(router_read, 1)
                dve.wait_ge(router_read, p + 1)
                link(dve.tensor_tensor(L[2], L[1], wide(st[:, 10, :]), ALU.mult))
                link(dve.tensor_tensor(L[0], L[2], weight("br").unsqueeze(1).broadcast_to([P, G, E]), ALU.add))

                def choose(src, top, picked):
                    link(dve.tensor_reduce(top, src, X, ALU.max))
                    link(dve.tensor_tensor(L[6], src, wide(top), ALU.is_equal))
                    link(dve.tensor_tensor(L[7], L[6], index, ALU.mult))
                    link(dve.tensor_reduce(rs[:, 5, :], L[7], X, ALU.max))
                    link(dve.tensor_tensor(picked, L[7], wide(rs[:, 5, :]), ALU.is_equal))

                choose(L[0], rs[:, 0, :], L[1])
                link(dve.tensor_scalar(L[2], L[1], -3e38, None, ALU.mult))
                link(dve.tensor_tensor(L[3], L[0], L[2], ALU.add))
                choose(L[3], rs[:, 1, :], L[4])
                dve.tensor_tensor(rs[:, 2, :], rs[:, 0, :], rs[:, 1, :], ALU.subtract).then_inc(gap_ready, 1)
                dve.wait_ge(tanh_ready, p + 1)
                link(dve.tensor_scalar(rs[:, 4, :], rs[:, 3, :], 0.5, 0.5, ALU.mult, ALU.add))
                link(dve.tensor_scalar(rs[:, 5, :], rs[:, 3, :], -0.5, 0.5, ALU.mult, ALU.add))
                link(dve.tensor_tensor(L[2], L[1], wide(rs[:, 4, :]), ALU.mult))
                link(dve.tensor_tensor(L[5], L[4], wide(rs[:, 5, :]), ALU.mult))
                link(dve.tensor_tensor(L[6], L[2], L[5], ALU.add))
                link(dve.tensor_copy(gate_parts[:, :, 0, :], L[6]))
                dve.tensor_tensor(gate_parts[:, :, 1, :], L[6], gate_parts[:, :, 0, :], ALU.subtract).then_inc(gparts_ready, 1)

            ybank = [SC[:, 0:CHUNK], SC[:, CHUNK:N]]
            fbank = SD[:, CHUNK:N]
            x1f = x1[:, :, :].rearrange("p a n -> p (a n)")

            def gated(i, b, m, first):
                dve.wait_ge(w2_done, (2 * i + b) * 4 + m + 1)
                dve.wait_ge(gb_ready, (2 * i + b) * 4 + m + 1)
                if m == 0:
                    if not first:
                        dve.wait_ge(fold_done, 2 * i + b - 1)
                    dst = acc[:, b, :]
                else:
                    dst = term[:, :]
                dve.scalar_tensor_tensor(dst, ybank[m % 2], b2t[:, m:m + 1], gate_b[:, m % 2, :], ALU.add,
                                         ALU.mult).then_inc(term_done, 1)
                dve.wait_ge(term_done, (2 * i + b) * 4 + m + 1)
                if m:
                    a = dve.tensor_tensor(acc[:, b, :], acc[:, b, :], term[:, :], ALU.add)
                    if m < E // 2 - 1:
                        a.then_inc(add_done, 1)
                        dve.wait_ge(add_done, (2 * i + b) * 2 + m)
                    else:
                        a.then_inc(acc_ready, 1)

            def finish(i):
                dve.wait_ge(fold_done, 2 * i + 2)
                part = x1f[:, bass.ds(i * CHUNK, CHUNK)]
                dve.tensor_tensor(part, fbank, part, ALU.add).then_inc(res_ready, 1)

            def step(i, first):
                for b in range(B2):
                    for m in range(E // 2):
                        gated(i, b, m, first)
                    if b == 0 and not first:
                        finish(i - 1)

            step(0, True)
            with dve.Fori(1, STEPS) as i:
                step(i, False)
            finish(STEPS - 1)


def kernel(**inputs):
    import concourse.bacc as bacc
    from concourse.bass_utils import run_bass_kernel_spmd

    nc = bacc.Bacc("TRN2", target_bir_lowering=False, num_devices=1)
    a = {n: np.asarray(v) for n, v in inputs.items()}
    const32, const16 = constants()
    arrays = {
        "in_x": np.ascontiguousarray(a["x"].transpose(0, 1, 3, 2)),
        "in_small": small_weights(a), "in_W1": a["L0_ffn_W1"], "in_W2": a["L0_ffn_W2"],
        "const32": const32, "const16": const16,
    }
    args = [nc.dram_tensor(n, a.shape, mybir.dt.from_np(a.dtype), kind="ExternalInput").ap() for n, a in arrays.items()]
    out = nc.dram_tensor("block_out", (PAIRS * B2, H, C, W), F32, kind="ExternalOutput").ap()
    metaformer(nc, *args, out)
    r = run_bass_kernel_spmd(nc, [arrays], core_ids=[0])
    return r.results[0]["block_out"].transpose(0, 1, 3, 2)
```

```python
from contextlib import ExitStack

import numpy as np

import concourse.bass as bass
from concourse import mybir

P = 128
PAIRS, B2, H, W, C = 2, 2, 64, 64, 16
K = 8
WW = W // K
G = B2 * (H // K)
HEADS, DH = 4, 16
HD = HEADS * DH
E, HID = 8, 256
KT = HID // P
NT = E * KT
CP = C // 2
N = W * C
TT = N // P
CHUNK = 512
STEPS = PAIRS * N // CHUNK
LN1_EPS, LN_EPS, NORM_EPS = 1e-6, 1e-5, 1e-12

F32 = mybir.dt.float32
F16 = mybir.dt.float16
I32 = mybir.dt.int32
ALU = mybir.AluOpType
ACT = mybir.ActivationFunctionType
X = mybir.AxisListType.X

TURN = {
    "dct_over_h": 0, "square_columns": 3, "norm_columns": 4, "dct_over_w": 8, "keep_dw": 11, "windows": 12,
    "keep_xd": 13, "conv_in": 14, "gelu_in": 16, "places": 17, "keep_xt": 18, "gram_matrices": 19,
    "mask_gram": 22, "gram_times_w": 24, "products": 26, "keep_tk": 27, "norms": 28, "inverse_norms": 31,
    "logits": 32, "depthwise": 33, "spread": 38, "gelu_depthwise": 40, "join": 41, "norms_of_k": 42,
    "softmax_in": 44, "conv_out": 45, "gelu_out": 46, "high": 47, "exponent": 48, "softmax_out": 50,
    "project": 52, "keep_y": 54, "heads": 55, "keep_yt": 56, "times_wv": 57, "mask_mix": 59, "low": 61,
    "mix_branches": 63, "to_frequencies": 66, "keep_back": 67, "inverse_over_kh": 68, "keep_half": 70,
    "inverse_over_kw": 71, "residual": 73, "tokens": 74, "centre_tokens": 75, "square_tokens": 77,
    "norm_tokens": 78, "high_part": 82, "low_part": 83, "features": 85, "keep_tokens": 86, "router": 88,
    "route": 89, "tanh_gap": 94, "shares": 95, "gates_to_rows": 98, "keep_gates": 99,
}
BEHIND = 5


def in_turn(*stages):
    return sorted(((TURN[f.__name__] + BEHIND * p, p, f) for f in stages for p in range(PAIRS)), key=lambda t: t[:2])


CONST = {}
at = 0
for name, n in (("dct_h", P), ("dct_w", P), ("idct_h", P), ("idct_w", P), ("ident", P), ("fold", H),
                ("shifted", (WW + 2) * C), ("diagonal", DH), ("small_index", E)):
    CONST[name] = slice(at, at + n)
    at += n
CONST_N = at


def constants():
    def twice(a):
        return np.kron(np.eye(2), a)
    n = np.arange(H)
    angle = np.cos(np.pi * (2 * n[None, :] + 1) * n[:, None] / (2 * H))
    dct = 2.0 * angle
    weight = np.ones(H)
    weight[0] = 0.5
    idct = (weight[:, None] * angle / H).T
    centred = dct - dct.mean(axis=1, keepdims=True)
    centred[1:] = dct[1:]
    centred[0] = 0.0
    block = np.zeros((P, (WW + 2) * C))
    for p in range(P):
        block[p, (p // C + 1) * C:(p // C + 2) * C] = 1
    out = np.zeros((P, CONST_N), np.float32)
    out[:, CONST["dct_h"]] = twice(centred.T)
    out[:, CONST["dct_w"]] = twice(dct.T)
    out[:, CONST["idct_h"]] = twice(idct.T)
    out[:, CONST["idct_w"]] = twice(idct.T)
    out[:, CONST["ident"]] = np.eye(P)
    out[:, CONST["fold"]] = np.tile(np.eye(H), (2, 1))
    out[:, CONST["shifted"]] = block
    out[:, CONST["diagonal"]] = np.tile(np.eye(DH), (P // DH, 1))
    out[:, CONST["small_index"]] = np.arange(E, 0, -1)[None, :]
    half = np.zeros((P, P + E // 2 * P), np.float16)
    half[:, :P] = np.eye(P)
    for r in range(2 * E):
        e = r % E
        half[r, P + (e // 2) * P + (e % 2) * H:P + (e // 2) * P + (e % 2) * H + H] = 1
    return out, half


SMALL = {}
at = 0
for name, n in (("wqk", 2 * HD), ("proj", HEADS * C), ("c1a", C), ("c2", C), ("wv_t", 2 * C), ("taps", 9), ("proj_b", 1),
                ("rescale", HEADS), ("ln_g", E), ("ln_b", E), ("b1", NT), ("b2", E // 2), ("wr", E), ("br", E),
                ("coef", H * K)):
    SMALL[name] = slice(at, at + n)
    at += n
SMALL_N = at


def small_weights(a):
    out = np.empty((P, SMALL_N), np.float32)

    def put(name, v):
        v = v.reshape(v.shape[0], -1)
        out[:, SMALL[name]] = np.tile(v, (P // v.shape[0], 1))
    put("wqk", np.concatenate([a["L0_conv_Wq"], a["L0_conv_Wk"]], axis=1))
    put("proj", a["L0_conv_proj_w"].reshape(HEADS, DH, C).transpose(1, 0, 2))
    put("c1a", a["L0_conv_c1a_w"].reshape(C, C).T)
    put("c2", a["L0_conv_c2_w"].reshape(C, C).T)
    wv = np.zeros((2, HD, 2, C), np.float32)
    for odd in range(2):
        wv[odd, :, odd] = a["L0_conv_Wv"].T
    put("wv_t", wv.reshape(P, 2 * C))
    put("taps", a["L0_conv_c1b_w"].reshape(C, 9))
    put("proj_b", a["L0_conv_proj_b"].reshape(C, 1))
    put("rescale", a["L0_conv_rescale"].reshape(1, HEADS))
    put("ln_g", a["L0_ffn_ln_g"].T)
    put("ln_b", a["L0_ffn_ln_b"].T)
    put("b1", a["L0_ffn_b1"].reshape(NT, P).T)
    put("b2", a["L0_ffn_b2"].reshape(E // 2, 2 * H).T)
    put("wr", a["L0_ffn_Wr"])
    put("br", a["L0_ffn_br"].reshape(1, E))
    put("coef", np.repeat(a["L0_conv_coef_emb"].reshape(H, WW, K).transpose(1, 0, 2), C, axis=0))
    return out


def metaformer(nc, x, small, W1, W2, const32, const16, out):
    ctx = ExitStack()
    with ctx:
        def sb(name, shape, dt=F32):
            return ctx.enter_context(nc.sbuf_tensor(name, shape, dt))

        def sem(name):
            return ctx.enter_context(nc.semaphore(name))

        psum = ctx.enter_context(nc.psum_tensor("psum", [P, 4, N], F32))
        SLOT = [psum[:, i, :] for i in range(4)]
        SA, SB_, SC, SD = SLOT

        def slot(p, n):
            return SLOT[2 * p + n]

        c32 = sb("c32", [P, CONST_N])
        c16 = sb("c16", [P, P + E // 2 * P], F16)

        def const(name):
            return c32[:, CONST[name]]
        dct_h, dct_w, idct_h, idct_w, ident = (const(n) for n in ("dct_h", "dct_w", "idct_h", "idct_w", "ident"))
        mask = c32[:, CONST["shifted"].start + C:CONST["shifted"].start + C + P]
        ident16 = c16[:, 0:P]
        gate_rows = [c16[0:2 * E, P + m * P:P + (m + 1) * P] for m in range(E // 2)]
        sm = sb("sm", [P, SMALL_N])

        def weight(name):
            return sm[:, SMALL[name]]
        wqk = weight("wqk").rearrange("p (a n) -> p a n", a=2)
        proj = weight("proj").rearrange("p (h c) -> p h c", h=HEADS)
        c1a, c2, wv_t, taps = weight("c1a"), weight("c2"), weight("wv_t"), weight("taps")
        lng, lnb, b1t, b2t = weight("ln_g"), weight("ln_b"), weight("b1"), weight("b2")
        coef = weight("coef")
        wq_bd = sb("wq_bd", [P, HEADS, P])
        proj_bd = sb("proj_bd", [P, HEADS, P])
        conv_bd = sb("conv_bd", [P, 4, P])
        wv_rep = sb("wv_rep", [P, 2, P])
        w1f = sb("w1f", [P, E, HID])
        w1g = sb("w1g", [P, E, HID])
        w1s = sb("w1s", [P, 2, E, HID], F16)
        w2 = sb("w2", [P, NT, H])
        b1p = sb("b1p", [P, NT])
        wrs = sb("wrs", [P, 2 * E], F16)

        xs = sb("xs", [P, PAIRS, N])
        x1 = sb("x1", [P, PAIRS, N])
        tok = sb("tok", [P, PAIRS, 2, B2, TT // 2 * P], F16)
        gates = sb("gates", [2 * E, PAIRS, 2, B2, TT // 2 * P], F16)
        h_pad = sb("h_pad", [P, PAIRS, B2, H + 2, K + 2])
        place = [sb(f"place{n}", [P, PAIRS, N]) for n in range(6)]
        wide = [sb(f"wide{n}", [P, PAIRS, 2 * N]) for n in range(2)]
        st = sb("st", [P, PAIRS, 16, G])
        root = sb("root", [P, PAIRS, 4, 2 * G * HEADS])
        row = sb("row", [P, PAIRS, 3, HEADS * G])
        gate_parts = sb("gate_parts", [P, PAIRS, G, 2, E], F16)

        xd = [place[0][:, p, :] for p in range(PAIRS)]
        x_out = xd
        xc = xd
        squares = [place[1][:, p, :] for p in range(PAIRS)]
        dw = squares
        logit = squares
        dh = [place[2][:, p, :] for p in range(PAIRS)]
        xt = dh
        norm_k = dh
        x_conv = [place[3][:, p, :] for p in range(PAIRS)]
        rest = x_conv
        back = x_conv
        parts = [x_conv[p].bitcast(F16) for p in range(PAIRS)]
        h2 = [place[4][:, p, :] for p in range(PAIRS)]
        half_back = h2
        lg = [h2[p].rearrange("p (n g e) -> p n g e", n=8, e=E) for p in range(PAIRS)]
        tk = [place[5][:, p, :] for p in range(PAIRS)]
        attn = tk
        gram = [wide[0][:, p, :].rearrange("p (g n) -> p g n", n=P) for p in range(PAIRS)]
        spread_k = [wide[0][:, p, 0:N] for p in range(PAIRS)]
        y_sb = [wide[0][:, p, 0:N] for p in range(PAIRS)]
        y_t = [wide[0][:, p, N:2 * N] for p in range(PAIRS)]
        prod = [wide[1][:, p, :].rearrange("p (g a n) -> p g a n", a=2, n=HD) for p in range(PAIRS)]
        own = [wide[1][:, p, :] for p in range(PAIRS)]
        mix = [wide[1][:, p, :].rearrange("p (g n) -> p g n", n=P) for p in range(PAIRS)]
        tap_bd = sb("tap_bd", [P, 9, P])

        hid = sb("hid", [P, 4, KT * CHUNK])
        gate_b = sb("gate_b", [P, 2, CHUNK])
        term = sb("term", [P, CHUNK])
        acc = sb("acc", [P, 2, CHUNK])

        x_in = [sem(f"x{p}_in") for p in range(PAIRS)]
        const_in, const16_in, weights_in = sem("const_in"), sem("const16_in"), sem("weights_in")
        ffn_in, out_done = sem("ffn_in"), sem("out_done")
        dve_chain, pool_chain = sem("dve_chain"), sem("pool_chain")
        pad_zero, bd_ready, w1_ready = sem("pad_zero"), sem("bd_ready"), sem("w1_ready")
        bias_t, bias_ready, wr_ready = sem("bias_t"), sem("bias_ready"), sem("wr_ready")
        names = ("dct_h_done dct_w_done xd_done c1a_done halo_done xt_done gram_done t_done norms_done "
                 "logit_done dconv_done spread_done c2_done y_done yt_done mix_done low_done back_done ih_done iw_done "
                 "tokens_done tok_done router_done gates_done").split()
        (dct_h_done, dct_w_done, xd_done, c1a_done, halo_done, xt_done, gram_done, t_done, norms_done,
         logit_done, dconv_done, spread_done, c2_done, y_done, yt_done, mix_done, low_done, back_done, ih_done, iw_done,
         tokens_done, tok_done, router_done, gates_done) = (sem(n) for n in names)
        names = ("sq_ready dh_ready dw_ready xd_ready xt_ready gram_ready tk_ready prod_ready own_ready "
                 "norms_ready spread_ready norm_k_ready logit_ready exp_ready attn_ready y_ready yt_ready mix_ready h1_ready "
                 "halo_ready dconv_ready xconv_ready h2_ready rest_ready xout_ready back_ready half_ready "
                 "x1_ready centred csq_ready xn_ready high_ready parts_ready tok_ready gap_ready tanh_ready "
                 "gparts_ready gates_ready router_read").split()
        (sq_ready, dh_ready, dw_ready, xd_ready, xt_ready, gram_ready, tk_ready, prod_ready, own_ready,
         norms_ready, spread_ready, norm_k_ready, logit_ready, exp_ready, attn_ready, y_ready, yt_ready, mix_ready, h1_ready,
         halo_ready, dconv_ready, xconv_ready, h2_ready, rest_ready, xout_ready, back_ready, half_ready,
         x1_ready, centred, csq_ready, xn_ready, high_ready, parts_ready, tok_ready, gap_ready, tanh_ready,
         gparts_ready, gates_ready, router_read) = (sem(n) for n in names)
        w1_done, gelu_ready, w2_done, gb_done, gb_ready, term_done, acc_ready, fold_done, res_ready, add_done = (
            sem(n) for n in ("w1_done gelu_ready w2_done gb_done gb_ready term_done acc_ready fold_done "
                             "res_ready add_done").split())

        block = ctx.enter_context(nc.Block())

        @block.sync
        def _(sp):
            xv = x.rearrange("(p b) h c w -> p (b h) (c w)", b=B2)
            sp.dma_start(xs[:, 0, :], xv[0]).then_inc(x_in[0], 16)
            sp.dma_start(c32[:, :], const32).then_inc(const_in, 16)
            sp.dma_start(sm[:, :], small).then_inc(weights_in, 16)
            sp.dma_start(xs[:, 1, :], xv[1]).then_inc(x_in[1], 16)
            sp.dma_start(c16[:, :], const16).then_inc(const16_in, 16)
            w1v = W1.rearrange("e d n -> d e n")
            for half in range(2):
                sp.dma_start(w1f[half * H:(half + 1) * H], w1v).then_inc(ffn_in, 16)
            sp.dma_start(w2[:, :, :], W2.rearrange("e (k p) d -> p (e k) d", p=P)).then_inc(ffn_in, 16)
            for i in range(STEPS):
                sp.wait_ge(res_ready, i + 1)
                pair, part = divmod(i, 2)
                view = out[B2 * pair:B2 * pair + B2].rearrange("b h c w -> (b h) (c w)")
                sp.dma_start(view[:, part * CHUNK:(part + 1) * CHUNK], x1[:, pair, part * CHUNK:(part + 1) * CHUNK]).then_inc(out_done, 16)
            sp.wait_ge(out_done, 16 * STEPS)

        @block.tensor
        def _(pe):
            def dct_over_h(p):
                pe.wait_ge(x_in[p], 16)
                pe.wait_ge(const_in, 16)
                for cp in range(CP):
                    mm = pe.matmul(slot(p, 0)[:, cp * P:(cp + 1) * P], xs[:, p, cp * P:(cp + 1) * P], dct_h, start=True, stop=True)
                mm.then_inc(dct_h_done, 1)

            def dct_over_w(p):
                pe.wait_ge(dh_ready, p + 1)
                for cp in range(CP):
                    mm = pe.matmul(slot(p, 1)[:, cp * P:(cp + 1) * P], dh[p][:, cp * P:(cp + 1) * P], dct_w, start=True, stop=True)
                mm.then_inc(dct_w_done, 1)

            def windows(p):
                pe.wait_ge(dw_ready, p + 1)
                for k2 in range(K):
                    mm = pe.transpose(slot(p, 0)[:, k2 * P:(k2 + 1) * P], dw[p][:, k2 * P:(k2 + 1) * P], ident)
                mm.then_inc(xd_done, 1)

            def conv_in(p):
                pe.wait_ge(xd_ready, p + 1)
                pe.wait_ge(bd_ready, 1)
                for j in range(2):
                    mm = pe.matmul(slot(p, 1)[:, j * CHUNK:(j + 1) * CHUNK], conv_bd[:, 0, :], xd[p][:, j * CHUNK:(j + 1) * CHUNK],
                                   start=True, stop=True)
                mm.then_inc(c1a_done, 1)
                edge = xd[p].rearrange("p (n k) -> p n k", k=K)
                pe.matmul(slot(p, 0)[:, 0:P], conv_bd[:, 1, :], edge[:, :, K - 1], start=True, stop=True)
                pe.matmul(slot(p, 0)[:, CHUNK:CHUNK + P], conv_bd[:, 2, :], edge[:, :, 0], start=True, stop=True).then_inc(halo_done, 1)

            def places(p):
                pe.wait_ge(h1_ready, p + 1)
                for q in range(K):
                    mm = pe.transpose(slot(p, 1)[:, q * P:(q + 1) * P], xd[p][:, q * P:(q + 1) * P], ident)
                mm.then_inc(xt_done, 1)

            def gram_matrices(p):
                pe.wait_ge(halo_ready, p + 1)
                pe.wait_ge(xt_ready, p + 1)
                for q in range(K):
                    for odd in range(2):
                        v = xt[p][odd * H:(odd + 1) * H, q * P:(q + 1) * P]
                        mm = pe.matmul(slot(p, odd)[:, q * P:(q + 1) * P], v, v, start=True, stop=True)
                mm.then_inc(gram_done, 1)

            def gram_times_w(p):
                pe.wait_ge(gram_ready, 2 * (p + 1))
                pe.wait_ge(weights_in, 16)
                wqk_all = wqk[:, :, :].rearrange("p a n -> p (a n)")
                for g in range(G):
                    mm = pe.matmul(slot(p, g // K)[:, g % K * P:(g % K + 1) * P], gram[p][:, g, :], wqk_all, start=True, stop=True)
                    if g % K == K - 1:
                        mm.then_inc(t_done, 1)

            def norms(p):
                pe.wait_ge(prod_ready, 2 * (p + 1))
                pe.wait_ge(tk_ready, 2 * (p + 1))
                for a in range(2):
                    for j in range(2):
                        mm = pe.matmul(slot(p, a)[:, j * CHUNK:(j + 1) * CHUNK], mask, prod[p][:, j * K:(j + 1) * K, a, :],
                                       start=True, stop=True)
                    mm.then_inc(norms_done, 1)

            def logits(p):
                pe.wait_ge(own_ready, 2 * (p + 1))
                for h in range(HEADS):
                    mm = pe.matmul(slot(p, 0)[:, h * G * DH:(h + 1) * G * DH], wq_bd[:, h, :],
                                   tk[p][:, h * G * DH:(h + 1) * G * DH], start=True, stop=True)
                mm.then_inc(logit_done, 1)

            def depthwise(p):
                for b in range(B2):
                    for tap in range(9):
                        mm = pe.matmul(slot(p, 1)[:, b * CHUNK:(b + 1) * CHUNK], tap_bd[:, tap, :],
                                       h_pad[:, p, b, tap // 3:tap // 3 + H, tap % 3:tap % 3 + K], start=tap == 0, stop=tap == 8)
                mm.then_inc(dconv_done, 1)

            def norms_of_k(p):
                pe.wait_ge(dconv_ready, p + 1)
                pe.wait_ge(spread_ready, p + 1)
                for j in range(2):
                    mm = pe.matmul(slot(p, 1)[:, j * CHUNK:(j + 1) * CHUNK], mask, spread_k[p][:, j * CHUNK:(j + 1) * CHUNK],
                                   start=True, stop=True)
                mm.then_inc(spread_done, 1)

            def conv_out(p):
                pe.wait_ge(norm_k_ready, p + 1)
                pe.wait_ge(xconv_ready, p + 1)
                for j in range(2):
                    mm = pe.matmul(slot(p, 1)[:, j * CHUNK:(j + 1) * CHUNK], conv_bd[:, 3, :], x_conv[p][:, j * CHUNK:(j + 1) * CHUNK],
                                   start=True, stop=True)
                mm.then_inc(c2_done, 1)

            def project(p):
                pe.wait_ge(attn_ready, p + 1)
                for h in range(HEADS):
                    mm = pe.matmul(slot(p, 0)[:, h * G * DH:(h + 1) * G * DH], proj_bd[:, h, :],
                                   attn[p][:, h * G * DH:(h + 1) * G * DH], start=True, stop=True)
                mm.then_inc(y_done, 1)

            def heads(p):
                pe.wait_ge(h2_ready, p + 1)
                pe.wait_ge(y_ready, p + 1)
                for q in range(K):
                    mm = pe.transpose(slot(p, 1)[:, q * P:(q + 1) * P], y_sb[p][:, q * P:(q + 1) * P], ident)
                mm.then_inc(yt_done, 1)

            def times_wv(p):
                pe.wait_ge(yt_ready, p + 1)
                for odd in range(2):
                    for j in range(2):
                        mm = pe.matmul(slot(p, odd)[:, j * CHUNK:(j + 1) * CHUNK], wv_rep[:, odd, :],
                                       y_t[p][:, j * CHUNK:(j + 1) * CHUNK], start=True, stop=True)
                    mm.then_inc(mix_done, 1)

            def low(p):
                pe.wait_ge(mix_ready, 2 * (p + 1))
                for g in range(G):
                    mm = pe.matmul(slot(p, 0)[:, g * H:(g + 1) * H], mix[p][:, g, :], xd[p][:, g * H:(g + 1) * H], start=True, stop=True)
                mm.then_inc(low_done, 1)

            def to_frequencies(p):
                pe.wait_ge(xout_ready, p + 1)
                for k2 in range(K):
                    mm = pe.transpose(slot(p, 1)[:, k2 * P:(k2 + 1) * P], x_out[p][:, k2 * P:(k2 + 1) * P], ident)
                mm.then_inc(back_done, 1)

            def inverse_over_kh(p):
                pe.wait_ge(back_ready, p + 1)
                for cp in range(CP):
                    mm = pe.matmul(slot(p, 0)[:, cp * P:(cp + 1) * P], back[p][:, cp * P:(cp + 1) * P], idct_h, start=True, stop=True)
                mm.then_inc(ih_done, 1)

            def inverse_over_kw(p):
                pe.wait_ge(half_ready, p + 1)
                for cp in range(CP):
                    mm = pe.matmul(slot(p, 1)[:, cp * P:(cp + 1) * P], half_back[p][:, cp * P:(cp + 1) * P], idct_w, start=True, stop=True)
                mm.then_inc(iw_done, 1)

            def tokens(p):
                pe.wait_ge(x1_ready, p + 1)
                for j in range(TT):
                    mm = pe.transpose(slot(p, 0)[:, j * P:(j + 1) * P], x1[:, p, j * P:(j + 1) * P], ident)
                mm.then_inc(tokens_done, 1)

            def features(p):
                pe.wait_ge(const16_in, 16)
                pe.wait_ge(parts_ready, p + 1)
                to = slot(p, 1).bitcast(F16)
                for j in range(TT):
                    for b in range(B2):
                        a = (j // 4 * 2 + b) * CHUNK + j % 4 * P
                        mm = pe.transpose(to[:, a:a + P], parts[p][:, (j * 2 + b) * P:(j * 2 + b + 1) * P], ident16)
                    if j % 4 == 3:
                        mm.then_inc(tok_done, 1)

            def router(p):
                pe.wait_ge(tok_ready, 2 * (p + 1))
                pe.wait_ge(wr_ready, 1)
                for j in range(TT):
                    for b in range(B2):
                        t = j * B2 + b
                        mm = pe.matmul(slot(p, 0)[:, t * 2 * E:(t + 1) * 2 * E],
                                       tok[:, p, j // 4, b, j % 4 * P:(j % 4 + 1) * P], wrs[:, :], start=True, stop=True)
                mm.then_inc(router_done, 1)

            def gates_to_rows(p):
                pe.wait_ge(gparts_ready, p + 1)
                to = slot(p, 1).bitcast(F16)
                for j in range(TT):
                    for b in range(B2):
                        a = (j // 4 * 2 + b) * CHUNK + j % 4 * P
                        mm = pe.transpose(to[0:2 * E, a:a + P],
                                          gate_parts[:, p, j * B2 + b, :, :].rearrange("p a e -> p (a e)"), ident16)
                mm.then_inc(gates_done, 1)

            stages = (dct_over_h, dct_over_w, windows, conv_in, places, gram_matrices, gram_times_w, norms, logits, depthwise,
                      norms_of_k, conv_out, project, heads, times_wv, low, to_frequencies, inverse_over_kh,
                      inverse_over_kw, tokens, features, router, gates_to_rows)
            for _, p, stage in in_turn(*stages):
                stage(p)

            pe.wait_ge(ffn_in, 16 * 3)
            pe.wait_ge(router_read, PAIRS)
            for t in range(NT):
                mm = pe.matmul(SA[:, t:t + 1], w1f[0:H, t // KT, t % KT * P:(t % KT + 1) * P], lnb[0:H, t // KT:t // KT + 1],
                               start=True, stop=True)
            mm.then_inc(bias_t, 1)
            pe.wait_ge(bias_ready, 1)

            hbank = [SA, SB_]
            ybank = [SC[:, 0:CHUNK], SC[:, CHUNK:N]]
            gbank, fbank = SD[:, 0:CHUNK], SD[:, CHUNK:N]
            tokf = tok[:, :, :, :, :].rearrange("p a j b n -> p (a j b n)")
            gatef = gates[:, :, :, :, :].rearrange("p a j b n -> p (a j b n)")

            def up(i, b, e, first):
                if not (first and b == 0 and e < 2):
                    pe.wait_ge(gelu_ready, (2 * i + b) * E + e - 1)
                for k in range(KT):
                    for part in range(2):
                        mm = pe.matmul(hbank[e % 2][:, k * CHUNK:(k + 1) * CHUNK], w1s[:, part, e, k * P:(k + 1) * P],
                                       tokf[:, bass.ds((2 * i + b) * CHUNK, CHUNK)], start=part == 0, stop=part == 1)
                mm.then_inc(w1_done, 1)

            def gate(i, b, m):
                pe.matmul(gbank, gate_rows[m], gatef[:, bass.ds((2 * i + b) * CHUNK, CHUNK)], start=True,
                          stop=True).then_inc(gb_done, 1)

            def down(i, b, m, first):
                pe.wait_ge(gb_ready, (2 * i + b) * 4 + m + 1)
                pe.wait_ge(gelu_ready, (2 * i + b) * E + 2 * m + 2)
                if not (first and b == 0 and m < 2):
                    pe.wait_ge(term_done, (2 * i + b) * 4 + m - 1)
                for k in range(KT):
                    for odd in range(2):
                        mm = pe.matmul(ybank[m % 2][odd * H:(odd + 1) * H, :], w2[:, (2 * m + odd) * KT + k, :],
                                       hid[:, (2 * m + odd) % 4, k * CHUNK:(k + 1) * CHUNK], start=k == 0, stop=k == KT - 1)
                mm.then_inc(w2_done, 1)

            def fold(i, b, first=False):
                pe.wait_ge(acc_ready, 2 * i + b + 1)
                if b == 0 and not first:
                    pe.wait_ge(res_ready, i)
                pe.matmul(fbank[b * H:(b + 1) * H, :], const("fold"), acc[:, b, :], start=True, stop=True).then_inc(fold_done, 1)

            def step(i, first):
                for b in range(B2):
                    up(i, b, 0, first)
                    up(i, b, 1, first)
                    if b == 1:
                        fold(i, 0, first)
                    elif not first:
                        fold(i - 1, 1)
                    for m in range(E // 2):
                        gate(i, b, m)
                        if m < E // 2 - 1:
                            up(i, b, 2 * m + 2, first)
                            up(i, b, 2 * m + 3, first)
                        down(i, b, m, first)

            pe.wait_ge(gates_ready, PAIRS)
            pe.wait_ge(w1_ready, 1)
            step(0, True)
            with pe.Fori(1, STEPS) as i:
                step(i, False)
            fold(STEPS - 1, 1)

        @block.scalar
        def _(act):
            def square_columns(p):
                act.wait_ge(dct_h_done, p + 1)
                act.activation(squares[p], slot(p, 0), ACT.Square).then_inc(sq_ready, 1)

            def keep_dw(p):
                act.wait_ge(dct_w_done, p + 1)
                act.copy(dw[p].rearrange("p (k w c) -> p c w k", k=K, c=C),
                         slot(p, 1).rearrange("p (c w k) -> p c w k", c=C, k=K)).then_inc(dw_ready, 1)

            def keep_xd(p):
                act.wait_ge(xd_done, p + 1)
                act.copy(xd[p].rearrange("p (n k) -> p k n", k=K), slot(p, 0).rearrange("p (k n) -> p k n", k=K)).then_inc(xd_ready, 1)

            def gelu_in(p):
                act.wait_ge(pad_zero, 1)
                act.wait_ge(c1a_done, p + 1)
                for b in range(B2):
                    g = act.activation(h_pad[:, p, b, 1:H + 1, 1:K + 1],
                                       slot(p, 1)[:, b * CHUNK:(b + 1) * CHUNK].rearrange("p (h k) -> p h k", k=K), ACT.Gelu)
                g.then_inc(h1_ready, 1)
                act.wait_ge(halo_done, p + 1)
                act.activation(h_pad[:, p, :, 1:H + 1, 0], slot(p, 0)[:, 0:P].rearrange("p (b h) -> p b h", b=B2), ACT.Gelu)
                act.activation(h_pad[:, p, :, 1:H + 1, K + 1], slot(p, 0)[:, CHUNK:CHUNK + P].rearrange("p (b h) -> p b h", b=B2),
                               ACT.Gelu).then_inc(halo_ready, 1)

            def keep_xt(p):
                act.wait_ge(xt_done, p + 1)
                act.copy(xt[p], slot(p, 1)).then_inc(xt_ready, 1)

            def keep_tk(p):
                for j in range(2):
                    act.wait_ge(prod_ready, 2 * p + j + 1)
                    act.copy(tk[p].rearrange("p (h g e) -> p g h e", h=HEADS, e=DH)[:, j * K:(j + 1) * K, :, :],
                             slot(p, j).rearrange("p (g a h e) -> p g a h e", a=2, h=HEADS, e=DH)[:, :, 1, :, :]).then_inc(tk_ready, 1)

            def gelu_depthwise(p):
                act.wait_ge(dconv_done, p + 1)
                act.activation(x_conv[p], slot(p, 1), ACT.Gelu).then_inc(dconv_ready, 1)

            def gelu_out(p):
                act.wait_ge(c2_done, p + 1)
                act.activation(h2[p], slot(p, 1), ACT.Gelu).then_inc(h2_ready, 1)

            def exponent(p):
                act.wait_ge(logit_ready, p + 1)
                act.activation(attn[p], logit[p], ACT.Exp).then_inc(exp_ready, 1)

            def keep_y(p):
                act.wait_ge(y_done, p + 1)
                act.copy(y_sb[p].rearrange("p (g h e) -> p h g e", h=HEADS, e=DH),
                         slot(p, 0).rearrange("p (h g e) -> p h g e", h=HEADS, g=G)).then_inc(y_ready, 1)

            def keep_yt(p):
                act.wait_ge(yt_done, p + 1)
                act.copy(y_t[p], slot(p, 1)).then_inc(yt_ready, 1)

            def keep_back(p):
                act.wait_ge(back_done, p + 1)
                act.copy(back[p].rearrange("p (c w k) -> p k w c", c=C, k=K),
                         slot(p, 1).rearrange("p (k w c) -> p k w c", k=K, c=C)).then_inc(back_ready, 1)

            def keep_half(p):
                act.wait_ge(ih_done, p + 1)
                act.copy(half_back[p], slot(p, 0)).then_inc(half_ready, 1)

            def square_tokens(p):
                act.wait_ge(centred, p + 1)
                act.activation(squares[p], xc[p], ACT.Square).then_inc(csq_ready, 1)

            def high_part(p):
                act.wait_ge(xn_ready, p + 1)
                act.copy(parts[p].rearrange("p (t a h) -> p t a h", a=2, h=H)[:, :, 0, :],
                         xc[p].rearrange("p (t h) -> p t h", h=H)).then_inc(high_ready, 1)

            def keep_tokens(p):
                for j in range(2):
                    act.wait_ge(tok_done, 2 * p + j + 1)
                    act.copy(tok[:, p, j, :, :].rearrange("p b n -> p (b n)"),
                             slot(p, 1).bitcast(F16)[:, j * N:(j + 1) * N]).then_inc(tok_ready, 1)

            def tanh_gap(p):
                act.wait_ge(gap_ready, p + 1)
                act.activation(st[:, p, 14, :], st[:, p, 13, :], ACT.Tanh, scale=0.5).then_inc(tanh_ready, 1)

            def keep_gates(p):
                act.wait_ge(gates_done, p + 1)
                act.copy(gates[:, p, :, :, :].rearrange("p j b n -> p (j b n)"), slot(p, 1).bitcast(F16)[0:2 * E, 0:2 * N]).then_inc(gates_ready, 1)

            stages = (square_columns, keep_dw, keep_xd, gelu_in, keep_xt, keep_tk, gelu_depthwise, gelu_out, exponent,
                      keep_y, keep_yt, keep_back, keep_half, square_tokens, high_part, keep_tokens, tanh_gap, keep_gates)
            for _, p, stage in in_turn(*stages):
                stage(p)

            hbank = [SA, SB_]
            gbank = SD[:, 0:CHUNK]

            def gelu(i, b, e, first):
                act.wait_ge(w1_done, (2 * i + b) * E + e + 1)
                if not (first and b == 0 and e < 4):
                    act.wait_ge(w2_done, (2 * i + b) * 4 + e // 2 - 1)
                for k in range(KT):
                    a = act.activation(hid[:, e % 4, k * CHUNK:(k + 1) * CHUNK], hbank[e % 2][:, k * CHUNK:(k + 1) * CHUNK],
                                       ACT.Gelu, bias=b1p[:, e * KT + k:e * KT + k + 1])
                a.then_inc(gelu_ready, 1)

            def spread(i, b, m, first):
                act.wait_ge(gb_done, (2 * i + b) * 4 + m + 1)
                if not (first and b == 0 and m < 2):
                    act.wait_ge(term_done, (2 * i + b) * 4 + m - 1)
                act.copy(gate_b[:, m % 2, :], gbank).then_inc(gb_ready, 1)

            def step(i, first):
                for b in range(B2):
                    gelu(i, b, 0, first)
                    gelu(i, b, 1, first)
                    for m in range(E // 2):
                        spread(i, b, m, first)
                        if m < E // 2 - 1:
                            gelu(i, b, 2 * m + 2, first)
                            gelu(i, b, 2 * m + 3, first)

            act.wait_ge(bias_ready, 1)
            step(0, True)
            with act.Fori(1, STEPS) as i:
                step(i, False)

        @block.gpsimd
        def _(pool):
            pool.memset(h_pad[:, :, :, :], 0.0).then_inc(pad_zero, 1)
            pool.wait_ge(const_in, 16)
            pool.wait_ge(weights_in, 16)
            shifted = const("shifted").rearrange("p (b c) -> p b c", c=C)

            def diagonal(dst, src, blocks):
                return pool.tensor_tensor(dst.rearrange("p (b c) -> p b c", c=C), shifted[:, blocks:blocks + WW, :],
                                          src.unsqueeze(1).broadcast_to([P, WW, C]), ALU.mult)

            diagonal(conv_bd[:, 0, :], c1a, 1)
            diagonal(conv_bd[:, 1, :], c1a, 0)
            diagonal(conv_bd[:, 2, :], c1a, 2)
            diagonal(conv_bd[:, 3, :], c2, 1)
            for h in range(HEADS):
                diagonal(wq_bd[:, h, :], wqk[:, 0, h * DH:(h + 1) * DH], 1)
                diagonal(proj_bd[:, h, :], proj[:, h, :], 1)
            for tap in range(9):
                pool.tensor_tensor(tap_bd[:, tap, :], ident, taps[:, tap:tap + 1].broadcast_to([P, P]), ALU.mult)
            for odd in range(2):
                last = pool.tensor_copy(wv_rep[:, odd, :].rearrange("p (b c) -> p b c", c=C),
                                        wv_t[:, odd * C:(odd + 1) * C].unsqueeze(1).broadcast_to([P, WW, C]))
            last.then_inc(bd_ready, 1)
            links = [0]

            def link(ins):
                links[0] += 1
                ins.then_inc(pool_chain, 1)
                pool.wait_ge(pool_chain, links[0])

            pool.tensor_copy(wrs[:, 0:E], weight("wr")).then_inc(pool_chain, 1)
            links[0] += 1
            pool.wait_ge(pool_chain, links[0])
            pool.tensor_tensor(wrs[:, E:2 * E], weight("wr"), wrs[:, 0:E], ALU.subtract).then_inc(wr_ready, 1)

            def spread(p):
                pool.wait_ge(norms_ready, p + 1)
                pool.tensor_tensor(spread_k[p].rearrange("p (g d) -> p g d", d=DH),
                                   root[:, p, 1, G * HEADS:].unsqueeze(2).broadcast_to([P, G * HEADS, DH]),
                                   const("diagonal").unsqueeze(1).broadcast_to([P, G * HEADS, DH]), ALU.mult).then_inc(spread_ready, 1)

            def join(p):
                pool.wait_ge(dconv_ready, p + 1)
                pool.tensor_tensor(x_conv[p], x_conv[p], xd[p], ALU.add).then_inc(xconv_ready, 1)

            def high(p):
                pool.wait_ge(h2_ready, p + 1)
                link(pool.tensor_tensor(h2[p], h2[p], x_conv[p], ALU.add))
                link(pool.tensor_tensor(rest[p], h2[p], xd[p], ALU.add))
                link(pool.tensor_tensor(h2[p].rearrange("p (b n) -> p b n", b=B2), h2[p].rearrange("p (b n) -> p b n", b=B2),
                                        coef.unsqueeze(1).broadcast_to([P, B2, CHUNK]), ALU.mult))
                pool.tensor_tensor(rest[p], rest[p], h2[p], ALU.subtract).then_inc(rest_ready, 1)

            def low_part(p):
                pool.wait_ge(high_ready, p + 1)
                v = parts[p].rearrange("p (t a h) -> p t a h", a=2, h=H)
                pool.tensor_tensor(v[:, :, 1, :], xc[p].rearrange("p (t h) -> p t h", h=H), v[:, :, 0, :],
                                   ALU.subtract).then_inc(parts_ready, 1)

            for _, p, stage in in_turn(spread, join, high, low_part):
                if stage is low_part and p == 0:
                    pool.wait_ge(ffn_in, 16 * 3)
                    link(pool.tensor_tensor(w1g[:, :, :], w1f[:, :, :], lng.unsqueeze(2).broadcast_to([P, E, HID]), ALU.mult))
                    link(pool.tensor_copy(w1s[:, 0, :, :], w1g[:, :, :]))
                    pool.tensor_tensor(w1s[:, 1, :, :], w1g[:, :, :], w1s[:, 0, :, :], ALU.subtract).then_inc(w1_ready, 1)
                stage(p)

        @block.vector
        def _(dve):
            links = [0]

            def link(ins):
                links[0] += 1
                ins.then_inc(dve_chain, 1)
                dve.wait_ge(dve_chain, links[0])

            def flat(t):
                return t.rearrange("p a b -> p (a b)")

            def inverse_root(dst, src, tmp):
                link(dve.tensor_scalar(tmp.bitcast(I32), src.bitcast(I32), 1, None, ALU.logical_shift_right))
                link(dve.tensor_scalar(dst.bitcast(I32), tmp.bitcast(I32), -1.0, float(0x5F3759DF), ALU.mult, ALU.add))
                for _ in range(3):
                    link(dve.scalar_tensor_tensor(tmp, dst, -0.5, src, ALU.mult, ALU.mult))
                    link(dve.tensor_tensor(tmp, tmp, dst, ALU.mult))
                    link(dve.scalar_tensor_tensor(dst, tmp, 1.5, dst, ALU.add, ALU.mult))

            def split(v, n):
                return v.rearrange("p (g h) -> p g h", h=n)

            def over(v, n, of=None):
                return v.unsqueeze(2).broadcast_to([P, v.shape[1], n])

            def norm_columns(p):
                s = st[:, p]
                dve.wait_ge(sq_ready, p + 1)
                link(dve.tensor_reduce(s[:, 0, :], split(squares[p], H), X, ALU.add))
                link(dve.tensor_scalar(s[:, 1, :], s[:, 0, :], 1.0 / (2 * H * H), LN1_EPS, ALU.mult, ALU.add))
                inverse_root(s[:, 2, :], s[:, 1, :], s[:, 3, :])
                dve.tensor_tensor(split(dh[p], H), split(slot(p, 0), H), over(s[:, 2, :], H), ALU.mult).then_inc(dh_ready, 1)

            def mask_gram(p):
                dve.wait_ge(gram_done, p + 1)
                gv = gram[p].rearrange("p (q o) n -> p q o n", o=2)
                for odd in range(2):
                    dve.tensor_tensor(gv[:, :, odd, :], split(slot(p, odd), P), mask.unsqueeze(1).broadcast_to([P, K, P]),
                                      ALU.mult).then_inc(gram_ready, 1)

            def products(p):
                for j in range(2):
                    dve.wait_ge(t_done, 2 * p + j + 1)
                    dve.tensor_tensor(prod[p][:, j * K:(j + 1) * K, :, :].rearrange("p g a n -> p g (a n)"), split(slot(p, j), P),
                                      wqk[:, :, :].rearrange("p a n -> p (a n)").unsqueeze(1).broadcast_to([P, K, P]),
                                      ALU.mult).then_inc(prod_ready, 1)

            def inverse_norms(p):
                dve.wait_ge(norms_done, 2 * (p + 1))
                for a in range(2):
                    dve.tensor_tensor(split(own[p][:, a * N:(a + 1) * N], DH), split(slot(p, a), DH),
                                      const("diagonal").unsqueeze(1).broadcast_to([P, G * HEADS, DH]), ALU.mult).then_inc(own_ready, 1)
                dve.wait_ge(own_ready, 2 * (p + 1))
                r = root[:, p]
                link(dve.tensor_reduce(r[:, 0, :], split(own[p], DH), X, ALU.add))
                link(dve.tensor_scalar(r[:, 3, :], r[:, 0, :], NORM_EPS ** 2, None, ALU.max))
                inverse_root(r[:, 1, :], r[:, 3, :], r[:, 2, :])
                dve.tensor_tensor(r[:, 0, 0:G * HEADS].rearrange("p (g h) -> p g h", h=HEADS),
                                  r[:, 1, 0:G * HEADS].rearrange("p (g h) -> p g h", h=HEADS),
                                  weight("rescale").unsqueeze(1).broadcast_to([P, G, HEADS]), ALU.mult).then_inc(norms_ready, 1)

            def softmax_in(p):
                dve.wait_ge(spread_done, p + 1)
                dve.wait_ge(norms_ready, p + 1)
                dve.tensor_tensor(split(norm_k[p], DH), split(slot(p, 1), DH), over(root[:, p, 0, 0:G * HEADS], DH),
                                  ALU.mult).then_inc(norm_k_ready, 1)
                dve.wait_ge(norm_k_ready, p + 1)
                dve.wait_ge(logit_done, p + 1)
                link(dve.tensor_tensor(logit[p].rearrange("p (h g e) -> p h g e", h=HEADS, g=G),
                                       slot(p, 0).rearrange("p (h g e) -> p h g e", h=HEADS, g=G),
                                       norm_k[p].rearrange("p (g h e) -> p h g e", h=HEADS, e=DH), ALU.mult))
                link(dve.tensor_reduce(row[:, p, 0, :], split(logit[p], DH), X, ALU.max))
                dve.tensor_tensor(split(logit[p], DH), split(logit[p], DH), over(row[:, p, 0, :], DH),
                                  ALU.subtract).then_inc(logit_ready, 1)

            def softmax_out(p):
                dve.wait_ge(exp_ready, p + 1)
                link(dve.tensor_reduce(row[:, p, 1, :], split(attn[p], DH), X, ALU.add))
                link(dve.reciprocal(row[:, p, 2, :], row[:, p, 1, :]))
                dve.tensor_tensor(split(attn[p], DH), split(attn[p], DH), over(row[:, p, 2, :], DH), ALU.mult).then_inc(attn_ready, 1)

            def mask_mix(p):
                mv = mix[p].rearrange("p (q o) n -> p q o n", o=2)
                for odd in range(2):
                    dve.wait_ge(mix_done, 2 * p + odd + 1)
                    dve.tensor_tensor(mv[:, :, odd, :], split(slot(p, odd), P), mask.unsqueeze(1).broadcast_to([P, K, P]),
                                      ALU.mult).then_inc(mix_ready, 1)

            def mix_branches(p):
                dve.wait_ge(rest_ready, p + 1)
                dve.wait_ge(low_done, p + 1)
                for b in range(B2):
                    c = slice(b * CHUNK, (b + 1) * CHUNK)
                    last = dve.scalar_tensor_tensor(h2[p][:, c], slot(p, 0)[:, c], weight("proj_b"), coef, ALU.add, ALU.mult)
                    links[0] += 1
                    last.then_inc(dve_chain, 1)
                dve.wait_ge(dve_chain, links[0])
                dve.tensor_tensor(x_out[p].rearrange("p (k n) -> p k n", k=K), h2[p].rearrange("p (n k) -> p k n", k=K),
                                  rest[p].rearrange("p (n k) -> p k n", k=K), ALU.add).then_inc(xout_ready, 1)

            def residual(p):
                dve.wait_ge(iw_done, p + 1)
                dve.tensor_tensor(x1[:, p, :], slot(p, 1), xs[:, p, :], ALU.add).then_inc(x1_ready, 1)

            def centre_tokens(p):
                s = st[:, p]
                dve.wait_ge(tokens_done, p + 1)
                link(dve.tensor_reduce(s[:, 5, :], split(slot(p, 0), H), X, ALU.add))
                link(dve.tensor_scalar(s[:, 6, :], s[:, 5, :], 1.0 / H, None, ALU.mult))
                dve.tensor_tensor(split(xc[p], H), split(slot(p, 0), H), over(s[:, 6, :], H), ALU.subtract).then_inc(centred, 1)

            def norm_tokens(p):
                s = st[:, p]
                dve.wait_ge(csq_ready, p + 1)
                link(dve.tensor_reduce(s[:, 0, :], split(squares[p], H), X, ALU.add))
                link(dve.tensor_scalar(s[:, 1, :], s[:, 0, :], 1.0 / H, None, ALU.mult))
                link(dve.tensor_scalar(s[:, 2, :], s[:, 1, :], LN_EPS, None, ALU.add))
                link(dve.scalar_tensor_tensor(s[:, 3, :], s[:, 2, :], LN_EPS, s[:, 1, :], ALU.mult, ALU.add))
                two = lambda a: s[:, a:a + 2, :].rearrange("p a g -> p (a g)")
                inverse_root(two(4), two(2), two(6))
                dve.tensor_tensor(split(xc[p], H), split(xc[p], H), over(s[:, 5, :], H), ALU.mult).then_inc(xn_ready, 1)
                link(dve.tensor_tensor(s[:, 8, :], s[:, 4, :], s[:, 3, :], ALU.mult))
                link(dve.tensor_tensor(s[:, 10, :], s[:, 8, :], s[:, 5, :], ALU.mult))

            def route(p):
                s = st[:, p]
                L = [lg[p][:, n, :, :] for n in range(8)]
                index = const("small_index").unsqueeze(1).broadcast_to([P, G, E])
                dve.wait_ge(router_done, p + 1)
                rv = slot(p, 0)[:, 0:G * 2 * E].rearrange("p (t a e) -> p t a e", a=2, e=E)
                link(dve.tensor_copy(L[0], rv[:, :, 0, :]))
                dve.tensor_tensor(L[1], L[0], rv[:, :, 1, :], ALU.add).then_inc(router_read, 1)
                dve.wait_ge(router_read, p + 1)
                link(dve.tensor_tensor(L[2], L[1], over(s[:, 10, :], E), ALU.mult))
                link(dve.tensor_tensor(L[0], L[2], weight("br").unsqueeze(1).broadcast_to([P, G, E]), ALU.add))

                def choose(src, top, picked):
                    link(dve.tensor_reduce(top, src, X, ALU.max))
                    link(dve.tensor_tensor(L[6], src, over(top, E), ALU.is_equal))
                    link(dve.tensor_tensor(L[7], L[6], index, ALU.mult))
                    link(dve.tensor_reduce(s[:, 12, :], L[7], X, ALU.max))
                    link(dve.tensor_tensor(picked, L[7], over(s[:, 12, :], E), ALU.is_equal))

                choose(L[0], s[:, 9, :], L[1])
                link(dve.scalar_tensor_tensor(L[3], L[1], -3e38, L[0], ALU.mult, ALU.add))
                choose(L[3], s[:, 11, :], L[4])
                dve.tensor_tensor(s[:, 13, :], s[:, 9, :], s[:, 11, :], ALU.subtract).then_inc(gap_ready, 1)

            def shares(p):
                s = st[:, p]
                L = [lg[p][:, n, :, :] for n in range(8)]
                dve.wait_ge(tanh_ready, p + 1)
                link(dve.tensor_scalar(s[:, 15, :], s[:, 14, :], 0.5, 0.5, ALU.mult, ALU.add))
                link(dve.tensor_scalar(s[:, 12, :], s[:, 14, :], -0.5, 0.5, ALU.mult, ALU.add))
                link(dve.tensor_tensor(L[2], L[1], over(s[:, 15, :], E), ALU.mult))
                link(dve.tensor_tensor(L[5], L[4], over(s[:, 12, :], E), ALU.mult))
                link(dve.tensor_tensor(L[6], L[2], L[5], ALU.add))
                link(dve.tensor_copy(gate_parts[:, p, :, 0, :], L[6]))
                dve.tensor_tensor(gate_parts[:, p, :, 1, :], L[6], gate_parts[:, p, :, 0, :], ALU.subtract).then_inc(gparts_ready, 1)

            stages = (norm_columns, mask_gram, products, inverse_norms, softmax_in, softmax_out, mask_mix, mix_branches,
                      residual, centre_tokens, norm_tokens, route, shares)
            for _, p, stage in in_turn(*stages):
                stage(p)

            dve.wait_ge(weights_in, 16)
            dve.wait_ge(bias_t, 1)
            dve.tensor_tensor(b1p[:, :], SA[:, 0:NT], b1t, ALU.add).then_inc(bias_ready, 1)

            ybank = [SC[:, 0:CHUNK], SC[:, CHUNK:N]]
            fbank = SD[:, CHUNK:N]
            x1f = x1[:, :, :].rearrange("p a n -> p (a n)")

            def gated(i, b, m, first):
                dve.wait_ge(w2_done, (2 * i + b) * 4 + m + 1)
                dve.wait_ge(gb_ready, (2 * i + b) * 4 + m + 1)
                if m == 0:
                    if not first:
                        dve.wait_ge(fold_done, 2 * i + b - 1)
                    dst = acc[:, b, :]
                else:
                    dst = term[:, :]
                dve.scalar_tensor_tensor(dst, ybank[m % 2], b2t[:, m:m + 1], gate_b[:, m % 2, :], ALU.add,
                                         ALU.mult).then_inc(term_done, 1)
                dve.wait_ge(term_done, (2 * i + b) * 4 + m + 1)
                if m:
                    a = dve.tensor_tensor(acc[:, b, :], acc[:, b, :], term[:, :], ALU.add)
                    if m < E // 2 - 1:
                        a.then_inc(add_done, 1)
                        dve.wait_ge(add_done, (2 * i + b) * 2 + m)
                    else:
                        a.then_inc(acc_ready, 1)

            def finish(i):
                dve.wait_ge(fold_done, 2 * i + 2)
                part = x1f[:, bass.ds(i * CHUNK, CHUNK)]
                dve.tensor_tensor(part, fbank, part, ALU.add).then_inc(res_ready, 1)

            def step(i, first):
                for b in range(B2):
                    for m in range(E // 2):
                        gated(i, b, m, first)
                    if b == 0 and not first:
                        finish(i - 1)

            step(0, True)
            with dve.Fori(1, STEPS) as i:
                step(i, False)
            finish(STEPS - 1)


def kernel(**inputs):
    import concourse.bacc as bacc
    from concourse.bass_utils import run_bass_kernel_spmd

    nc = bacc.Bacc("TRN2", target_bir_lowering=False, num_devices=1)
    a = {n: np.asarray(v) for n, v in inputs.items()}
    const32, const16 = constants()
    arrays = {
        "in_x": np.ascontiguousarray(a["x"].transpose(0, 1, 3, 2)),
        "in_small": small_weights(a), "in_W1": a["L0_ffn_W1"], "in_W2": a["L0_ffn_W2"],
        "const32": const32, "const16": const16,
    }
    args = [nc.dram_tensor(n, a.shape, mybir.dt.from_np(a.dtype), kind="ExternalInput").ap() for n, a in arrays.items()]
    out = nc.dram_tensor("block_out", (PAIRS * B2, H, C, W), F32, kind="ExternalOutput").ap()
    metaformer(nc, *args, out)
    r = run_bass_kernel_spmd(nc, [arrays], core_ids=[0])
    return r.results[0]["block_out"].transpose(0, 1, 3, 2)
```

```python
from contextlib import ExitStack

import numpy as np

import concourse.bass as bass
from concourse import mybir

P = 128
PAIRS, B2, H, W, C = 2, 2, 64, 64, 16
K = 8
WW = W // K
G = B2 * (H // K)
HEADS, DH = 4, 16
HD = HEADS * DH
E, HID = 8, 256
KT = HID // P
NT = E * KT
CP = C // 2
N = W * C
TT = N // P
CHUNK = 512
STEPS = PAIRS * N // CHUNK
LN1_EPS, LN_EPS, NORM_EPS = 1e-6, 1e-5, 1e-12

F32 = mybir.dt.float32
F16 = mybir.dt.float16
I32 = mybir.dt.int32
ALU = mybir.AluOpType
ACT = mybir.ActivationFunctionType
X = mybir.AxisListType.X

TURN = {
    "dct_over_h": (0, 2), "square_columns": (1, 3), "dct_over_w": (4, 9), "windows": (5, 12), "conv_in": (6, 20),
    "keep_dw": (7, 11), "keep_xd": (8, 14), "gelu_in": (10, 16), "norm_columns": (13, 17), "places": (15, 21),
    "keep_xt": (18, 25), "join": (19, 38), "high": (22, 79), "gram_matrices": (23, 26), "gram_times_w": (24, 30),
    "first_taps": (27, 35), "norms": (28, 41), "mask_gram": (29, 34), "second_taps": (31, 50), "logits": (32, 52),
    "products": (33, 36), "keep_tk": (37, 45), "inverse_norms": (39, 46), "norms_of_k": (40, 55),
    "softmax_in": (42, 61), "gelu_second": (43, 57), "softmax_out": (44, 74), "gelu_depthwise": (47, 53),
    "gelu_out": (48, 68), "conv_out": (49, 63), "project": (51, 65), "exponent": (54, 66), "heads": (56, 69),
    "times_wv": (58, 72), "keep_y": (59, 70), "low": (60, 73), "mask_mix": (62, 81), "keep_yt": (64, 76),
    "to_frequencies": (67, 85), "inverse_over_kh": (71, 90), "keep_back": (75, 82), "keep_half": (77, 86),
    "square_tokens": (78, 92), "mix_branches": (80, 83), "inverse_over_kw": (84, 91), "high_part": (87, 100),
    "tokens": (88, 94), "residual": (89, 96), "norm_tokens": (93, 97), "keep_tokens": (95, 110), "features": (98, 103),
    "low_part": (99, 106), "router": (101, 113), "bias": (102, 102), "route": (104, 111), "gates_to_rows": (105, 118),
    "shares": (107, 116), "biases": (108, 108), "tanh_gap": (109, 115), "keep_gates": (112, 119),
}
UNIT_TURNS = (
    (114, 117, 120, 121, 122, 123, 124, 125, 126),
    (127, 128, 129, 130, 131, 132, 133, 134, 136),
)
UNITS = B2 * E // 2


def in_turn(stages, experts=None):
    turns = [(TURN[f.__name__][p], f, (p,)) for f in stages for p in range(PAIRS)]
    if experts:
        turns += [(UNIT_TURNS[i][v + 1], experts, (i, v)) for i in range(STEPS // PAIRS) for v in range(-1, UNITS)]
    return [(f, args) for _, f, args in sorted(turns, key=lambda t: t[0])]


CONST = {}
at = 0
for name, n in (("dct_h", P), ("dct_w", P), ("idct_h", P), ("idct_w", P), ("ident", P), ("fold", H),
                ("centre", P), ("pick", P + DH - 1),
                ("shifted", (WW + 2) * C), ("diagonal", DH), ("small_index", E)):
    CONST[name] = slice(at, at + n)
    at += n
CONST_N = at


def constants():
    def twice(a):
        return np.kron(np.eye(2), a)
    n = np.arange(H)
    angle = np.cos(np.pi * (2 * n[None, :] + 1) * n[:, None] / (2 * H))
    dct = 2.0 * angle
    weight = np.ones(H)
    weight[0] = 0.5
    idct = (weight[:, None] * angle / H).T
    centred = dct - dct.mean(axis=1, keepdims=True)
    centred[1:] = dct[1:]
    centred[0] = 0.0
    block = np.zeros((P, (WW + 2) * C))
    for p in range(P):
        block[p, (p // C + 1) * C:(p // C + 2) * C] = 1
    out = np.zeros((P, CONST_N), np.float32)
    out[:, CONST["dct_h"]] = twice(centred.T)
    out[:, CONST["dct_w"]] = twice(dct.T)
    out[:, CONST["idct_h"]] = twice(idct.T)
    out[:, CONST["idct_w"]] = twice(idct.T)
    out[:, CONST["ident"]] = np.eye(P)
    out[:, CONST["fold"]] = np.tile(np.eye(H), (2, 1))
    out[:, CONST["centre"]] = twice(np.eye(H) - 1.0 / H)
    for p in range(P):
        out[p, CONST["pick"].start + p // C * C + DH - 1] = 1
    out[:, CONST["shifted"]] = block
    out[:, CONST["diagonal"]] = np.tile(np.eye(DH), (P // DH, 1))
    out[:, CONST["small_index"]] = np.arange(E, 0, -1)[None, :]
    half = np.zeros((P, P + E // 2 * P), np.float16)
    half[:, :P] = np.eye(P)
    for r in range(2 * E):
        e = r % E
        half[r, P + (e // 2) * P + (e % 2) * H:P + (e // 2) * P + (e % 2) * H + H] = 1
    return out, half


SMALL = {}
at = 0
for name, n in (("wqk", 2 * HD), ("proj", HEADS * C), ("c1a", C), ("c2", C), ("wv_t", 2 * C), ("taps", 9), ("proj_b", 1),
                ("rescale", HEADS), ("ln_g", E), ("ln_b", E), ("b1", NT), ("b2", E // 2), ("wr", E), ("br", E),
                ("coef", H * K)):
    SMALL[name] = slice(at, at + n)
    at += n
SMALL_N = at


def small_weights(a):
    out = np.empty((P, SMALL_N), np.float32)

    def put(name, v):
        v = v.reshape(v.shape[0], -1)
        out[:, SMALL[name]] = np.tile(v, (P // v.shape[0], 1))
    put("wqk", np.concatenate([a["L0_conv_Wq"], a["L0_conv_Wk"]], axis=1))
    put("proj", a["L0_conv_proj_w"].reshape(HEADS, DH, C).transpose(1, 0, 2))
    put("c1a", a["L0_conv_c1a_w"].reshape(C, C).T)
    put("c2", a["L0_conv_c2_w"].reshape(C, C).T)
    wv = np.zeros((2, HD, 2, C), np.float32)
    for odd in range(2):
        wv[odd, :, odd] = a["L0_conv_Wv"].T
    put("wv_t", wv.reshape(P, 2 * C))
    put("taps", a["L0_conv_c1b_w"].reshape(C, 9))
    put("proj_b", a["L0_conv_proj_b"].reshape(C, 1))
    put("rescale", a["L0_conv_rescale"].reshape(1, HEADS))
    put("ln_g", a["L0_ffn_ln_g"].T)
    put("ln_b", a["L0_ffn_ln_b"].T)
    put("b1", a["L0_ffn_b1"].reshape(NT, P).T)
    put("b2", a["L0_ffn_b2"].reshape(E // 2, 2 * H).T)
    put("wr", a["L0_ffn_Wr"])
    put("br", a["L0_ffn_br"].reshape(1, E))
    put("coef", np.repeat(a["L0_conv_coef_emb"].reshape(H, WW, K).transpose(1, 0, 2), C, axis=0))
    return out


def metaformer(nc, x, small, W1, W2, const32, const16, out):
    ctx = ExitStack()
    with ctx:
        def sb(name, shape, dt=F32):
            return ctx.enter_context(nc.sbuf_tensor(name, shape, dt))

        def sem(name):
            return ctx.enter_context(nc.semaphore(name))

        psum = ctx.enter_context(nc.psum_tensor("psum", [P, 4, N], F32))
        SLOT = [psum[:, i, :] for i in range(4)]

        def slot(p, n):
            return SLOT[2 * p + n]

        def bank(v, j):
            return v[:, j * CHUNK:(j + 1) * CHUNK]

        def split(v, n):
            return v.rearrange("p (g h) -> p g h", h=n)

        def parity(g):
            return g // K * K + g % 2 * 4 + g % K // 2

        c32 = sb("c32", [P, CONST_N])
        c16 = sb("c16", [P, P + E // 2 * P], F16)

        def const(name):
            return c32[:, CONST[name]]
        dct_h, dct_w, idct_h, idct_w, ident = (const(n) for n in ("dct_h", "dct_w", "idct_h", "idct_w", "ident"))
        mask = c32[:, CONST["shifted"].start + C:CONST["shifted"].start + C + P]
        ident16 = c16[:, 0:P]
        gate_rows = [c16[0:2 * E, P + m * P:P + (m + 1) * P] for m in range(E // 2)]
        sm = sb("sm", [P, SMALL_N])

        def weight(name):
            return sm[:, SMALL[name]]
        wqk = weight("wqk").rearrange("p (a n) -> p a n", a=2)
        proj = weight("proj").rearrange("p (h c) -> p h c", h=HEADS)
        c1a, c2, wv_t, taps_w = weight("c1a"), weight("c2"), weight("wv_t"), weight("taps")
        lng, lnb, b1t, b2t = weight("ln_g"), weight("ln_b"), weight("b1"), weight("b2")
        coef = weight("coef")
        wq_bd = sb("wq_bd", [P, HEADS, P])
        proj_bd = sb("proj_bd", [P, HEADS, P])
        conv_bd = sb("conv_bd", [P, 4, P])
        tap_bd = sb("tap_bd", [P, 9, P])
        wv_rep = sb("wv_rep", [P, 2, P])
        coef_rest = sb("coef_rest", [P, CHUNK])
        w1f = sb("w1f", [P, E, HID])
        w1g = sb("w1g", [P, E, HID])
        w1s = sb("w1s", [P, 2, E, HID], F16)
        w2 = sb("w2", [P, NT, H])
        b1p = sb("b1p", [P, NT])
        wrs = sb("wrs", [P, 2 * E], F16)

        xs = sb("xs", [P, PAIRS, N])
        x1 = sb("x1", [P, PAIRS, N])
        tok = sb("tok", [P, PAIRS, 2, B2, TT // 2 * P], F16)
        gates = sb("gates", [2 * E, PAIRS, 2, B2, TT // 2 * P], F16)
        h_pad = sb("h_pad", [P, PAIRS, B2, H + 2, K + 2])
        place = [sb(f"place{n}", [P, PAIRS, N]) for n in range(6)]
        wide = [sb(f"wide{n}", [P, PAIRS, 2 * N]) for n in range(2)]
        st = sb("st", [P, PAIRS, 16, G])
        root = sb("root", [P, PAIRS, 4, 2 * G * HEADS])
        row = sb("row", [P, PAIRS, 3, HEADS * G])
        gate_parts = sb("gate_parts", [P, PAIRS, G, 2, E], F16)

        xd = [place[0][:, p, :] for p in range(PAIRS)]
        xc = xd
        squares = [place[1][:, p, :] for p in range(PAIRS)]
        dw = squares
        logit = squares
        dh = [place[2][:, p, :] for p in range(PAIRS)]
        xt = dh
        x_out = dh
        x_conv = [place[3][:, p, :] for p in range(PAIRS)]
        rest = x_conv
        back = x_conv
        parts = [x_conv[p].bitcast(F16) for p in range(PAIRS)]
        h2 = [place[4][:, p, :] for p in range(PAIRS)]
        half_back = h2
        lg = [h2[p].rearrange("p (n g e) -> p n g e", n=8, e=E) for p in range(PAIRS)]
        tk = [place[5][:, p, :] for p in range(PAIRS)]
        attn = tk
        gram = [wide[0][:, p, :].rearrange("p (g n) -> p g n", n=P) for p in range(PAIRS)]
        spread_k = [wide[0][:, p, 0:N] for p in range(PAIRS)]
        y_sb = [wide[0][:, p, 0:N] for p in range(PAIRS)]
        y_t = [wide[0][:, p, N:2 * N] for p in range(PAIRS)]
        prod = [wide[1][:, p, :].rearrange("p (g a n) -> p g a n", a=2, n=HD) for p in range(PAIRS)]
        mix = [wide[1][:, p, :].rearrange("p (g n) -> p g n", n=P) for p in range(PAIRS)]

        h_bank = [slot(0, 0)[:, odd * CHUNK:(odd + 1) * CHUNK] for odd in range(2)]
        y_bank, g_bank = slot(0, 1)[:, 0:CHUNK], slot(0, 1)[:, CHUNK:N]
        hid = sb("hid", [P, 2, 2 * KT, CHUNK])
        gate_b = sb("gate_b", [P, 2, CHUNK])
        term = sb("term", [P, CHUNK])
        acc = sb("acc", [P, 2, CHUNK])

        def part_of(p, part, j):
            return parts[p].rearrange("p (t a h) -> p t a h", a=2, h=H)[:, j * K:(j + 1) * K, part, :]

        def shifted(p, b, tap):
            return h_pad[:, p, b, tap // 3:tap // 3 + H, tap % 3:tap % 3 + K]

        x_in = [sem(f"x{p}_in") for p in range(PAIRS)]
        dct_in = sem("dct_in")
        const_in, const16_in, weights_in = sem("const_in"), sem("const16_in"), sem("weights_in")
        ffn_in, out_done = sem("ffn_in"), sem("out_done")
        dve_chain, pool_chain = sem("dve_chain"), sem("pool_chain")
        pad_zero, bd_ready, w1_ready = sem("pad_zero"), sem("bd_ready"), sem("w1_ready")
        conv_bd_ready = sem("conv_bd_ready")
        bias_t, bias_ready, wr_ready = sem("bias_t"), sem("bias_ready"), sem("wr_ready")
        (dct_h_done, dct_w_done, xd_done, c1a_done, halo_done, xt_done, gram_done, t_done, norms_done, logit_done, spread_done,
         c2_done, y_done, yt_done, mix_done, low_done, back_done, ih_done, iw_done, tokens_done, tok_done, router_done,
         gates_done) = (sem(n) for n in (
             "dct_h_done dct_w_done xd_done c1a_done halo_done xt_done gram_done t_done norms_done logit_done spread_done "
             "c2_done y_done yt_done mix_done low_done back_done ih_done iw_done tokens_done tok_done router_done "
             "gates_done").split())
        first_taps_done, second_taps_done = sem("first_taps_done"), sem("second_taps_done")
        second_dconv_ready = sem("second_dconv_ready")
        (sq_ready, dh_ready, dw_ready, xd_ready, h1_ready, halo_ready, xt_ready, gram_ready, prod_ready, tk_ready,
         dconv_ready, xconv_ready, spread_ready, scaled_ready, h2_ready, rest_ready, logit_ready, exp_ready,
         attn_ready, y_ready, yt_ready, mix_ready, xout_ready, back_ready, half_ready, x1_ready, csq_ready, xn_ready,
         high_ready, parts_ready, tok_ready, gap_ready, tanh_ready, gparts_ready, gates_ready, coef_ready) = (sem(n) for n in (
             "sq_ready dh_ready dw_ready xd_ready h1_ready halo_ready xt_ready gram_ready prod_ready tk_ready "
             "dconv_ready xconv_ready spread_ready scaled_ready h2_ready rest_ready logit_ready exp_ready "
             "attn_ready y_ready yt_ready mix_ready xout_ready back_ready half_ready x1_ready csq_ready xn_ready "
             "high_ready parts_ready tok_ready gap_ready tanh_ready gparts_ready gates_ready coef_ready").split())
        w1_done, gelu_ready, w2_done, gb_done, gb_ready, term_done, acc_ready, fold_done, res_ready, add_done = (
            sem(n) for n in ("w1_done gelu_ready w2_done gb_done gb_ready term_done acc_ready fold_done "
                             "res_ready add_done").split())

        block = ctx.enter_context(nc.Block())

        @block.sync
        def _(sp):
            xv = x.rearrange("(p b) h c w -> p (b h) (c w)", b=B2)
            sp.dma_start(c32[:, 0:P], const32[:, 0:P]).then_inc(dct_in, 16)
            sp.dma_start(xs[:, 0, :], xv[0]).then_inc(x_in[0], 16)
            sp.dma_start(c32[:, P:CONST_N], const32[:, P:CONST_N]).then_inc(const_in, 16)
            sp.dma_start(sm[:, :], small).then_inc(weights_in, 16)
            sp.dma_start(xs[:, 1, :], xv[1]).then_inc(x_in[1], 16)
            sp.dma_start(c16[:, :], const16).then_inc(const16_in, 16)
            w1v = W1.rearrange("e d n -> d e n")
            for half in range(2):
                sp.dma_start(w1f[half * H:(half + 1) * H], w1v).then_inc(ffn_in, 16)
            sp.dma_start(w2[:, :, :], W2.rearrange("e (k p) d -> p (e k) d", p=P)).then_inc(ffn_in, 16)
            for i in range(STEPS):
                sp.wait_ge(res_ready, i + 1)
                pair, part = divmod(i, 2)
                view = out[B2 * pair:B2 * pair + B2].rearrange("b h c w -> (b h) (c w)")
                sp.dma_start(view[:, part * CHUNK:(part + 1) * CHUNK], x1[:, pair, part * CHUNK:(part + 1) * CHUNK]).then_inc(out_done, 16)
            sp.wait_ge(out_done, 16 * STEPS)

        @block.tensor
        def _(pe):
            def dct_over_h(p):
                pe.wait_ge(x_in[p], 16)
                pe.wait_ge(dct_in, 16)
                for cp in range(CP):
                    mm = pe.matmul(slot(p, 0)[:, cp * P:(cp + 1) * P], xs[:, p, cp * P:(cp + 1) * P], dct_h, start=True, stop=True)
                    if cp % 4 == 3:
                        mm.then_inc(dct_h_done, 1)

            def dct_over_w(p):
                pe.wait_ge(const_in, 16)
                for cp in range(CP):
                    if cp % 4 == 0:
                        pe.wait_ge(dh_ready, 2 * p + cp // 4 + 1)
                    mm = pe.matmul(slot(p, 1)[:, cp * P:(cp + 1) * P], dh[p][:, cp * P:(cp + 1) * P], dct_w, start=True, stop=True)
                    if cp % 4 == 3:
                        mm.then_inc(dct_w_done, 1)

            def windows(p):
                pe.wait_ge(dw_ready, 2 * (p + 1))
                for k2 in range(K):
                    mm = pe.transpose(slot(p, 0)[:, k2 * P:(k2 + 1) * P], dw[p][:, k2 * P:(k2 + 1) * P], ident)
                    if k2 % 4 == 3:
                        mm.then_inc(xd_done, 1)

            def conv_in(p):
                pe.wait_ge(xd_ready, 2 * (p + 1))
                pe.wait_ge(conv_bd_ready, 1)
                for j in range(2):
                    pe.matmul(slot(p, 1)[:, j * CHUNK:(j + 1) * CHUNK], conv_bd[:, 0, :], xd[p][:, j * CHUNK:(j + 1) * CHUNK],
                              start=True, stop=True).then_inc(c1a_done, 1)
                edge = xd[p].rearrange("p (n k) -> p n k", k=K)
                pe.matmul(slot(p, 0)[:, 0:P], conv_bd[:, 1, :], edge[:, :, K - 1], start=True, stop=True)
                pe.matmul(slot(p, 0)[:, CHUNK:CHUNK + P], conv_bd[:, 2, :], edge[:, :, 0], start=True, stop=True).then_inc(halo_done, 1)

            def places(p):
                for q in range(K):
                    if q % 4 == 0:
                        pe.wait_ge(h1_ready, 2 * p + q // 4 + 1)
                    mm = pe.transpose(slot(p, 1)[:, q * P:(q + 1) * P], xd[p][:, q * P:(q + 1) * P], ident)
                    if q % 4 == 3:
                        mm.then_inc(xt_done, 1)

            def gram_matrices(p):
                pe.wait_ge(halo_ready, p + 1)
                for j in range(2):
                    pe.wait_ge(xt_ready, 2 * p + j + 1)
                    for q in range(4):
                        for odd in range(2):
                            v = xt[p][odd * H:(odd + 1) * H, (4 * j + q) * P:(4 * j + q + 1) * P]
                            mm = pe.matmul(slot(p, j)[:, (4 * odd + q) * P:(4 * odd + q + 1) * P], v, v, start=True, stop=True)
                    mm.then_inc(gram_done, 1)

            def gram_times_w(p):
                pe.wait_ge(weights_in, 16)
                wqk_all = wqk[:, :, :].rearrange("p a n -> p (a n)")
                for g in range(G):
                    if g % K == 0:
                        pe.wait_ge(gram_ready, 2 * p + g // K + 1)
                    mm = pe.matmul(slot(p, g // K)[:, g % K * P:(g % K + 1) * P], gram[p][:, parity(g), :], wqk_all, start=True, stop=True)
                    if g % K == K - 1:
                        mm.then_inc(t_done, 1)

            def norms(p):
                pe.wait_ge(tk_ready, 2 * p + 1)
                pe.wait_ge(prod_ready, 2 * (p + 1))
                columns = prod[p].rearrange("p g a (h d) -> p d (g a h)", d=DH)
                for d in range(DH):
                    mm = pe.matmul(slot(p, 0)[:, 0:2 * G * HEADS], const("pick")[:, DH - 1 - d:DH - 1 - d + P], columns[:, d, :],
                                   start=d == 0, stop=d == DH - 1)
                mm.then_inc(norms_done, 1)

            def logits(p):
                pe.wait_ge(tk_ready, 2 * (p + 1))
                pe.wait_ge(bd_ready, 1)
                for h in range(HEADS):
                    mm = pe.matmul(slot(p, 1)[:, h * G * DH:(h + 1) * G * DH], wq_bd[:, h, :],
                                   tk[p][:, h * G * DH:(h + 1) * G * DH], start=True, stop=True)
                mm.then_inc(logit_done, 1)

            def second_taps(p):
                pe.wait_ge(tk_ready, 2 * p + 1)
                pe.wait_ge(bd_ready, 1)
                for tap in range(9):
                    mm = pe.matmul(bank(slot(p, 0), 1), tap_bd[:, tap, :], shifted(p, 1, tap), start=tap == 0, stop=tap == 8)
                mm.then_inc(second_taps_done, 1)

            def norms_of_k(p):
                pe.wait_ge(spread_ready, p + 1)
                pe.wait_ge(second_dconv_ready, p + 1)
                for j in range(2):
                    mm = pe.matmul(slot(p, 0)[:, j * CHUNK:(j + 1) * CHUNK], mask, spread_k[p][:, j * CHUNK:(j + 1) * CHUNK],
                                   start=True, stop=True)
                mm.then_inc(spread_done, 1)

            def conv_out(p):
                pe.wait_ge(scaled_ready, p + 1)
                pe.wait_ge(xconv_ready, p + 1)
                for j in range(2):
                    pe.matmul(slot(p, 1)[:, j * CHUNK:(j + 1) * CHUNK], conv_bd[:, 3, :], x_conv[p][:, j * CHUNK:(j + 1) * CHUNK],
                              start=True, stop=True).then_inc(c2_done, 1)

            def project(p):
                for h in range(HEADS):
                    if h % 2 == 0:
                        pe.wait_ge(attn_ready, 2 * p + h // 2 + 1)
                    mm = pe.matmul(slot(p, 0)[:, h * G * DH:(h + 1) * G * DH], proj_bd[:, h, :],
                                   attn[p][:, h * G * DH:(h + 1) * G * DH], start=True, stop=True)
                    if h % 2:
                        mm.then_inc(y_done, 1)

            def heads(p):
                pe.wait_ge(h2_ready, 2 * (p + 1))
                pe.wait_ge(y_ready, 2 * (p + 1))
                for q in range(K):
                    mm = pe.transpose(slot(p, 1)[:, q * P:(q + 1) * P], y_sb[p][:, q * P:(q + 1) * P], ident)
                    if q % 4 == 3:
                        mm.then_inc(yt_done, 1)

            def times_wv(p):
                for j in range(2):
                    pe.wait_ge(yt_ready, 2 * p + j + 1)
                    for odd in range(2):
                        mm = pe.matmul(slot(p, j)[:, odd * CHUNK:(odd + 1) * CHUNK], wv_rep[:, odd, :],
                                       y_t[p][:, j * CHUNK:(j + 1) * CHUNK], start=True, stop=True)
                    mm.then_inc(mix_done, 1)

            def low(p):
                for g in range(G):
                    if g % K == 0:
                        pe.wait_ge(mix_ready, 2 * p + g // K + 1)
                    mm = pe.matmul(slot(p, 0)[:, g * H:(g + 1) * H], mix[p][:, parity(g), :], xd[p][:, g * H:(g + 1) * H], start=True, stop=True)
                    if g % K == K - 1:
                        mm.then_inc(low_done, 1)

            def to_frequencies(p):
                pe.wait_ge(xout_ready, 2 * (p + 1))
                for k2 in range(K):
                    mm = pe.transpose(slot(p, 1)[:, k2 * P:(k2 + 1) * P], x_out[p][:, k2 * P:(k2 + 1) * P], ident)
                    if k2 % 4 == 3:
                        mm.then_inc(back_done, 1)

            def inverse_over_kh(p):
                pe.wait_ge(back_ready, 2 * (p + 1))
                for cp in range(CP):
                    mm = pe.matmul(slot(p, 0)[:, cp * P:(cp + 1) * P], back[p][:, cp * P:(cp + 1) * P], idct_h, start=True, stop=True)
                    if cp % 4 == 3:
                        mm.then_inc(ih_done, 1)

            def inverse_over_kw(p):
                for cp in range(CP):
                    if cp % 4 == 0:
                        pe.wait_ge(half_ready, 2 * p + cp // 4 + 1)
                    mm = pe.matmul(slot(p, 1)[:, cp * P:(cp + 1) * P], half_back[p][:, cp * P:(cp + 1) * P], idct_w, start=True, stop=True)
                    if cp % 4 == 3:
                        mm.then_inc(iw_done, 1)

            def tokens(p):
                for j in range(TT):
                    if j % 4 == 0:
                        pe.wait_ge(x1_ready, 2 * p + j // 4 + 1)
                    mm = pe.matmul(slot(p, 0)[:, j * P:(j + 1) * P], x1[:, p, j * P:(j + 1) * P], const("centre"), start=True, stop=True)
                    if j % 4 == 3:
                        mm.then_inc(tokens_done, 1)

            def features(p):
                pe.wait_ge(const16_in, 16)
                to = slot(p, 1).bitcast(F16)
                for j in range(TT):
                    if j % 4 == 0:
                        pe.wait_ge(parts_ready, 2 * p + j // 4 + 1)
                    for b in range(B2):
                        a = (j // 4 * 2 + b) * CHUNK + j % 4 * P
                        mm = pe.transpose(to[:, a:a + P], parts[p][:, (j * 2 + b) * P:(j * 2 + b + 1) * P], ident16)
                    if j % 4 == 3:
                        mm.then_inc(tok_done, 1)

            def router(p):
                pe.wait_ge(wr_ready, 1)
                for j in range(TT):
                    if j % 4 == 0:
                        pe.wait_ge(tok_ready, 2 * p + j // 4 + 1)
                    for b in range(B2):
                        t = j * B2 + b
                        for part in range(2):
                            mm = pe.matmul(slot(p, 0)[:, t * E:(t + 1) * E], tok[:, p, j // 4, b, j % 4 * P:(j % 4 + 1) * P],
                                           wrs[:, part * E:(part + 1) * E], start=part == 0, stop=part == 1)
                mm.then_inc(router_done, 1)

            def gates_to_rows(p):
                pe.wait_ge(gparts_ready, p + 1)
                to = slot(p, 1).bitcast(F16)
                for j in range(TT):
                    for b in range(B2):
                        a = (j // 4 * 2 + b) * CHUNK + j % 4 * P
                        mm = pe.transpose(to[0:2 * E, a:a + P],
                                          gate_parts[:, p, j * B2 + b, :, :].rearrange("p a e -> p (a e)"), ident16)
                    if j % 4 == 3:
                        mm.then_inc(gates_done, 1)

            def bias(p):
                if p:
                    return
                pe.wait_ge(ffn_in, 16 * 3)
                pe.wait_ge(xn_ready, 2)
                for t in range(NT):
                    mm = pe.matmul(slot(0, 0)[:, CHUNK + t:CHUNK + t + 1], w1f[0:H, t // KT, t % KT * P:(t % KT + 1) * P],
                                   lnb[0:H, t // KT:t // KT + 1], start=True, stop=True)
                mm.then_inc(bias_t, 1)

            tokf = tok[:, :, :, :, :].rearrange("p a j b n -> p (a j b n)")
            gatef = gates[:, :, :, :, :].rearrange("p a j b n -> p (a j b n)")

            def chunk(i, v):
                return bass.ds((B2 * i + v // (E // 2)) * CHUNK, CHUNK)

            def first(i):
                return isinstance(i, int) and i == 0

            def up(i, v, k):
                u, m = UNITS * i + v, v % (E // 2)
                for odd in range(2):
                    if first(u) and k == 0:
                        pe.wait_ge(bias_ready, 1)
                        pe.wait_ge(gates_ready, 2)
                        pe.wait_ge(w1_ready, 1)
                    else:
                        pe.wait_ge(gelu_ready, 4 * u + 2 * k + odd - 1)
                        if k == 0 and odd == 0:
                            pe.wait_ge(gb_ready, u)
                            if v == 2 and not first(i):
                                pe.wait_ge(res_ready, i)
                    e = 2 * m + odd
                    for part in range(2):
                        mm = pe.matmul(h_bank[odd], w1s[:, part, e, k * P:(k + 1) * P], tokf[:, chunk(i, v)],
                                       start=part == 0, stop=part == 1)
                    mm.then_inc(w1_done, 1)

            def gate(i, v):
                pe.matmul(g_bank, gate_rows[v % (E // 2)], gatef[:, chunk(i, v)], start=True, stop=True).then_inc(gb_done, 1)

            def down(i, v, k):
                u, m = UNITS * i + v, v % (E // 2)
                pe.wait_ge(gelu_ready, 4 * u + 2 * k + 2)
                if k == 0 and not first(u):
                    pe.wait_ge(term_done, u)
                for odd in range(2):
                    mm = pe.matmul(y_bank[odd * H:(odd + 1) * H, :], w2[:, (2 * m + odd) * KT + k, :],
                                   hid[:, v % 2, 2 * k + odd, :], start=k == 0, stop=k == KT - 1)
                if k == KT - 1:
                    mm.then_inc(w2_done, 1)

            def fold(i, units):
                pe.wait_ge(acc_ready, B2 * (i + 1))
                pe.wait_ge(gb_ready, units)
                for b in range(B2):
                    mm = pe.matmul(g_bank[b * H:(b + 1) * H, :], const("fold"), acc[:, b, :], start=True, stop=True)
                mm.then_inc(fold_done, 1)

            def experts(i, v):
                if v == UNITS - 1:
                    return
                up(i, v + 1, 0)
                gate(i, v + 1)
                if v < 0:
                    if not first(i):
                        down(i - 1, UNITS - 1, 0)
                    up(i, v + 1, 1)
                    if not first(i):
                        down(i - 1, UNITS - 1, 1)
                elif v == 0 and not first(i):
                    up(i, v + 1, 1)
                    down(i, v, 0)
                    fold(i - 1, UNITS * i + 2)
                    down(i, v, 1)
                else:
                    down(i, v, 0)
                    up(i, v + 1, 1)
                    down(i, v, 1)

            stages = (dct_over_h, dct_over_w, windows, conv_in, places, gram_matrices, gram_times_w, norms, logits, second_taps,
                      norms_of_k, conv_out, project, heads, times_wv, low, to_frequencies, inverse_over_kh,
                      inverse_over_kw, tokens, features, router, bias, gates_to_rows)
            for stage, args in in_turn(stages, experts):
                stage(*args)
            pe.wait_ge(gates_ready, 2 * PAIRS)
            with pe.Fori(STEPS // PAIRS, STEPS) as i:
                for v in range(-1, UNITS):
                    experts(i, v)
            for k in range(KT):
                down(STEPS - 1, UNITS - 1, k)
            fold(STEPS - 1, UNITS * STEPS)

        @block.scalar
        def _(act):
            def square_columns(p):
                for j in range(2):
                    act.wait_ge(dct_h_done, 2 * p + j + 1)
                    act.activation(bank(squares[p], j), bank(slot(p, 0), j), ACT.Square).then_inc(sq_ready, 1)

            def keep_dw(p):
                for j in range(2):
                    act.wait_ge(dct_w_done, 2 * p + j + 1)
                    act.copy(dw[p].rearrange("p (k w c) -> p c w k", k=K, c=C)[:, j * K:(j + 1) * K],
                             bank(slot(p, 1), j).rearrange("p (c w k) -> p c w k", w=WW, k=K)).then_inc(dw_ready, 1)

            def keep_xd(p):
                for j in range(2):
                    act.wait_ge(xd_done, 2 * p + j + 1)
                    act.copy(xd[p].rearrange("p (n k) -> p k n", k=K)[:, 4 * j:4 * j + 4],
                             bank(slot(p, 0), j).rearrange("p (k n) -> p k n", n=P)).then_inc(xd_ready, 1)

            def gelu_in(p):
                act.wait_ge(pad_zero, 1)
                for b in range(B2):
                    act.wait_ge(c1a_done, 2 * p + b + 1)
                    act.activation(h_pad[:, p, b, 1:H + 1, 1:K + 1], bank(slot(p, 1), b).rearrange("p (h k) -> p h k", k=K),
                                   ACT.Gelu).then_inc(h1_ready, 1)
                act.wait_ge(halo_done, p + 1)
                act.activation(h_pad[:, p, :, 1:H + 1, 0], slot(p, 0)[:, 0:P].rearrange("p (b h) -> p b h", b=B2), ACT.Gelu)
                act.activation(h_pad[:, p, :, 1:H + 1, K + 1], slot(p, 0)[:, CHUNK:CHUNK + P].rearrange("p (b h) -> p b h", b=B2),
                               ACT.Gelu).then_inc(halo_ready, 1)

            def keep_xt(p):
                for j in range(2):
                    act.wait_ge(xt_done, 2 * p + j + 1)
                    act.copy(bank(xt[p], j), bank(slot(p, 1), j)).then_inc(xt_ready, 1)

            def keep_tk(p):
                for j in range(2):
                    act.wait_ge(prod_ready, 2 * p + j + 1)
                    act.copy(tk[p].rearrange("p (h g e) -> p g h e", h=HEADS, e=DH)[:, j * K:(j + 1) * K, :, :],
                             slot(p, j).rearrange("p (g a h e) -> p g a h e", a=2, h=HEADS, e=DH)[:, :, 1, :, :]).then_inc(tk_ready, 1)

            def gelu_depthwise(p):
                act.wait_ge(first_taps_done, p + 1)
                act.activation(bank(x_conv[p], 0), bank(x_conv[p], 0), ACT.Gelu).then_inc(dconv_ready, 1)

            def gelu_second(p):
                act.wait_ge(second_taps_done, p + 1)
                act.activation(bank(x_conv[p], 1), bank(slot(p, 0), 1), ACT.Gelu).then_inc(second_dconv_ready, 1)

            def gelu_out(p):
                for j in range(2):
                    act.wait_ge(c2_done, 2 * p + j + 1)
                    act.activation(bank(h2[p], j), bank(slot(p, 1), j), ACT.Gelu).then_inc(h2_ready, 1)

            def exponent(p):
                for j in range(2):
                    act.wait_ge(logit_ready, 2 * p + j + 1)
                    act.activation(bank(attn[p], j), bank(logit[p], j), ACT.Exp).then_inc(exp_ready, 1)

            def keep_y(p):
                for j in range(2):
                    act.wait_ge(y_done, 2 * p + j + 1)
                    act.copy(y_sb[p].rearrange("p (g h e) -> p h g e", h=HEADS, e=DH)[:, 2 * j:2 * j + 2],
                             bank(slot(p, 0), j).rearrange("p (h g e) -> p h g e", g=G, e=DH)).then_inc(y_ready, 1)

            def keep_yt(p):
                for j in range(2):
                    act.wait_ge(yt_done, 2 * p + j + 1)
                    act.copy(bank(y_t[p], j), bank(slot(p, 1), j)).then_inc(yt_ready, 1)

            def keep_back(p):
                for j in range(2):
                    act.wait_ge(back_done, 2 * p + j + 1)
                    act.copy(back[p].rearrange("p (c w k) -> p k w c", c=C, k=K)[:, 4 * j:4 * j + 4],
                             bank(slot(p, 1), j).rearrange("p (k w c) -> p k w c", w=WW, c=C)).then_inc(back_ready, 1)

            def keep_half(p):
                for j in range(2):
                    act.wait_ge(ih_done, 2 * p + j + 1)
                    act.copy(bank(half_back[p], j), bank(slot(p, 0), j)).then_inc(half_ready, 1)

            def square_tokens(p):
                for j in range(2):
                    act.wait_ge(tokens_done, 2 * p + j + 1)
                    act.activation(bank(squares[p], j), bank(slot(p, 0), j), ACT.Square).then_inc(csq_ready, 1)

            def high_part(p):
                for j in range(2):
                    act.wait_ge(xn_ready, 2 * p + j + 1)
                    act.copy(part_of(p, 0, j), split(bank(xc[p], j), H)).then_inc(high_ready, 1)

            def keep_tokens(p):
                for j in range(2):
                    act.wait_ge(tok_done, 2 * p + j + 1)
                    act.copy(tok[:, p, j, :, :].rearrange("p b n -> p (b n)"),
                             slot(p, 1).bitcast(F16)[:, j * N:(j + 1) * N]).then_inc(tok_ready, 1)

            def tanh_gap(p):
                act.wait_ge(gap_ready, p + 1)
                act.activation(st[:, p, 14, :], st[:, p, 13, :], ACT.Tanh, scale=0.5).then_inc(tanh_ready, 1)

            def keep_gates(p):
                for j in range(2):
                    act.wait_ge(gates_done, 2 * p + j + 1)
                    act.copy(gates[:, p, j, :, :].rearrange("p b n -> p (b n)"),
                             slot(p, 1).bitcast(F16)[0:2 * E, j * N:(j + 1) * N]).then_inc(gates_ready, 1)

            def experts(i, v):
                v += 1
                if v == UNITS:
                    return
                u, m = UNITS * i + v, v % (E // 2)
                early = isinstance(u, int) and u < 2
                for t in range(2 * KT):
                    k, odd = divmod(t, 2)
                    act.wait_ge(w1_done, 4 * u + t + 1)
                    if t == 0 and not early:
                        act.wait_ge(w2_done, u - 1)
                    e = 2 * m + odd
                    act.activation(hid[:, v % 2, t, :], h_bank[odd], ACT.Gelu,
                                   bias=b1p[:, e * KT + k:e * KT + k + 1]).then_inc(gelu_ready, 1)
                    if t == 1:
                        act.wait_ge(gb_done, u + 1)
                        if not early:
                            act.wait_ge(term_done, u - 1)
                        act.copy(gate_b[:, v % 2, :], g_bank).then_inc(gb_ready, 1)

            stages = (square_columns, keep_dw, keep_xd, gelu_in, keep_xt, keep_tk, gelu_depthwise, gelu_second, gelu_out, exponent,
                      keep_y, keep_yt, keep_back, keep_half, square_tokens, high_part, keep_tokens, tanh_gap, keep_gates)
            for stage, args in in_turn(stages, experts):
                stage(*args)
            with act.Fori(STEPS // PAIRS, STEPS) as i:
                for v in range(-1, UNITS):
                    experts(i, v)

        @block.gpsimd
        def _(pool):
            pool.memset(h_pad[:, :, :, :], 0.0).then_inc(pad_zero, 1)
            pool.wait_ge(const_in, 16)
            pool.wait_ge(weights_in, 16)
            blocks_of = const("shifted").rearrange("p (b c) -> p b c", c=C)

            def diagonal(dst, src, blocks):
                return pool.tensor_tensor(dst.rearrange("p (b c) -> p b c", c=C), blocks_of[:, blocks:blocks + WW, :],
                                          src.unsqueeze(1).broadcast_to([P, WW, C]), ALU.mult)

            diagonal(conv_bd[:, 0, :], c1a, 1)
            diagonal(conv_bd[:, 1, :], c1a, 0)
            diagonal(conv_bd[:, 2, :], c1a, 2)
            diagonal(conv_bd[:, 3, :], c2, 1).then_inc(conv_bd_ready, 1)
            for h in range(HEADS):
                diagonal(wq_bd[:, h, :], wqk[:, 0, h * DH:(h + 1) * DH], 1)
                diagonal(proj_bd[:, h, :], proj[:, h, :], 1)
            for tap in range(9):
                pool.tensor_tensor(tap_bd[:, tap, :], ident, taps_w[:, tap:tap + 1].broadcast_to([P, P]), ALU.mult)
            for odd in range(2):
                last = pool.tensor_copy(wv_rep[:, odd, :].rearrange("p (b c) -> p b c", c=C),
                                        wv_t[:, odd * C:(odd + 1) * C].unsqueeze(1).broadcast_to([P, WW, C]))
            last.then_inc(bd_ready, 1)
            links = [0]

            def link(ins):
                links[0] += 1
                ins.then_inc(pool_chain, 1)
                pool.wait_ge(pool_chain, links[0])

            pool.tensor_copy(wrs[:, 0:E], weight("wr")).then_inc(pool_chain, 1)
            links[0] += 1
            pool.wait_ge(pool_chain, links[0])
            pool.tensor_tensor(wrs[:, E:2 * E], weight("wr"), wrs[:, 0:E], ALU.subtract).then_inc(wr_ready, 1)

            def join(p):
                pool.wait_ge(dconv_ready, p + 1)
                pool.wait_ge(second_dconv_ready, p + 1)
                pool.tensor_tensor(x_conv[p], x_conv[p], xd[p], ALU.add).then_inc(xconv_ready, 1)

            def high(p):
                pool.wait_ge(h2_ready, 2 * (p + 1))
                pool.wait_ge(coef_ready, 1)
                link(pool.tensor_tensor(h2[p], h2[p], x_conv[p], ALU.add))
                link(pool.tensor_tensor(h2[p].rearrange("p (b n) -> p b n", b=B2), h2[p].rearrange("p (b n) -> p b n", b=B2),
                                        coef_rest[:, :].unsqueeze(1).broadcast_to([P, B2, CHUNK]), ALU.mult))
                pool.tensor_tensor(rest[p], h2[p], xd[p], ALU.add).then_inc(rest_ready, 1)

            def low_part(p):
                for j in range(2):
                    pool.wait_ge(high_ready, 2 * p + j + 1)
                    pool.tensor_tensor(part_of(p, 1, j), split(bank(xc[p], j), H), part_of(p, 0, j), ALU.subtract).then_inc(parts_ready, 1)

            for stage, (p,) in in_turn((join, high, low_part)):
                stage(p)
                if stage is high and p == PAIRS - 1:
                    pool.wait_ge(ffn_in, 16 * 3)
                    link(pool.tensor_tensor(w1g[:, :, :], w1f[:, :, :], lng.unsqueeze(2).broadcast_to([P, E, HID]), ALU.mult))
                    link(pool.tensor_copy(w1s[:, 0, :, :], w1g[:, :, :]))
                    pool.tensor_tensor(w1s[:, 1, :, :], w1g[:, :, :], w1s[:, 0, :, :], ALU.subtract).then_inc(w1_ready, 1)

        @block.vector
        def _(dve):
            links = [0]

            def count(ins):
                links[0] += 1
                ins.then_inc(dve_chain, 1)

            def link(ins):
                count(ins)
                dve.wait_ge(dve_chain, links[0])

            def inverse_root(dst, src, tmp):
                link(dve.tensor_scalar(dst.bitcast(I32), src.bitcast(I32), -0.5, float(0x5F3759DF), ALU.mult, ALU.add))
                for _ in range(3):
                    link(dve.scalar_tensor_tensor(tmp, dst, -0.5, src, ALU.mult, ALU.mult))
                    link(dve.tensor_tensor(tmp, tmp, dst, ALU.mult))
                    link(dve.scalar_tensor_tensor(dst, tmp, 1.5, dst, ALU.add, ALU.mult))

            def over(v, n):
                return v.unsqueeze(2).broadcast_to([P, v.shape[1], n])

            dve.wait_ge(weights_in, 16)
            dve.tensor_scalar(coef_rest[:, :], coef, -1.0, 1.0, ALU.mult, ALU.add).then_inc(coef_ready, 1)

            def norm_columns(p):
                s = st[:, p]
                for j in range(2):
                    dve.wait_ge(sq_ready, 2 * p + j + 1)
                    (count, link)[j](dve.tensor_reduce(s[:, 0, j * K:(j + 1) * K], split(bank(squares[p], j), H), X, ALU.add))
                link(dve.tensor_scalar(s[:, 1, :], s[:, 0, :], 1.0 / (2 * H * H), LN1_EPS, ALU.mult, ALU.add))
                inverse_root(s[:, 2, :], s[:, 1, :], s[:, 3, :])
                for j in range(2):
                    dve.tensor_tensor(split(bank(dh[p], j), H), split(bank(slot(p, 0), j), H), over(s[:, 2, j * K:(j + 1) * K], H),
                                      ALU.mult).then_inc(dh_ready, 1)

            def first_taps(p):
                dve.wait_ge(halo_ready, p + 1)
                dst = bank(x_conv[p], 0).rearrange("p (h k) -> p h k", k=K)
                link(dve.tensor_scalar(dst, shifted(p, 0, 0), taps_w[:, 0:1], None, ALU.mult))
                for tap in range(1, 9):
                    last = dve.scalar_tensor_tensor(dst, shifted(p, 0, tap), taps_w[:, tap:tap + 1], dst, ALU.mult, ALU.add)
                    if tap < 8:
                        link(last)
                last.then_inc(first_taps_done, 1)

            def mask_gram(p):
                for j in range(2):
                    dve.wait_ge(gram_done, 2 * p + j + 1)
                    dve.tensor_tensor(gram[p][:, j * K:(j + 1) * K, :], split(slot(p, j), P), mask.unsqueeze(1).broadcast_to([P, K, P]),
                                      ALU.mult).then_inc(gram_ready, 1)

            def products(p):
                for j in range(2):
                    dve.wait_ge(t_done, 2 * p + j + 1)
                    dve.tensor_tensor(prod[p][:, j * K:(j + 1) * K, :, :].rearrange("p g a n -> p g (a n)"), split(slot(p, j), P),
                                      wqk[:, :, :].rearrange("p a n -> p (a n)").unsqueeze(1).broadcast_to([P, K, P]),
                                      ALU.mult).then_inc(prod_ready, 1)

            def inverse_norms(p):
                r = root[:, p]
                dve.wait_ge(norms_done, p + 1)
                link(dve.tensor_scalar(r[:, 3, :], slot(p, 0)[:, 0:2 * G * HEADS], NORM_EPS ** 2, None, ALU.max))
                inverse_root(r[:, 1, :], r[:, 3, :], r[:, 2, :])
                both = r[:, 1, :].rearrange("p (g a h) -> p a g h", a=2, h=HEADS)
                dve.tensor_tensor(spread_k[p].rearrange("p (g h d) -> p g h d", h=HEADS, d=DH),
                                  both[:, 1, :, :].unsqueeze(3).broadcast_to([P, G, HEADS, DH]),
                                  const("diagonal").unsqueeze(1).unsqueeze(1).broadcast_to([P, G, HEADS, DH]),
                                  ALU.mult).then_inc(spread_ready, 1)
                link(dve.tensor_tensor(r[:, 0, 0:G * HEADS].rearrange("p (h g) -> p g h", h=HEADS), both[:, 0, :, :],
                                       weight("rescale").unsqueeze(1).broadcast_to([P, G, HEADS]), ALU.mult))
                dve.wait_ge(logit_done, p + 1)
                dve.tensor_tensor(split(logit[p], DH), split(slot(p, 1), DH), over(r[:, 0, 0:G * HEADS], DH),
                                  ALU.mult).then_inc(scaled_ready, 1)

            def softmax_in(p):
                dve.wait_ge(scaled_ready, p + 1)
                dve.wait_ge(spread_done, p + 1)
                link(dve.tensor_tensor(logit[p].rearrange("p (h g e) -> p h g e", h=HEADS, g=G),
                                       logit[p].rearrange("p (h g e) -> p h g e", h=HEADS, g=G),
                                       slot(p, 0).rearrange("p (g h e) -> p h g e", h=HEADS, e=DH), ALU.mult))
                for j in range(2):
                    top = row[:, p, 0, 2 * j * G:2 * (j + 1) * G]
                    link(dve.tensor_reduce(top, split(bank(logit[p], j), DH), X, ALU.max))
                    dve.tensor_tensor(split(bank(logit[p], j), DH), split(bank(logit[p], j), DH), over(top, DH),
                                      ALU.subtract).then_inc(logit_ready, 1)

            def softmax_out(p):
                for j in range(2):
                    part = slice(2 * j * G, 2 * (j + 1) * G)
                    dve.wait_ge(exp_ready, 2 * p + j + 1)
                    link(dve.tensor_reduce(row[:, p, 1, part], split(bank(attn[p], j), DH), X, ALU.add))
                    link(dve.reciprocal(row[:, p, 2, part], row[:, p, 1, part]))
                    dve.tensor_tensor(split(bank(attn[p], j), DH), split(bank(attn[p], j), DH), over(row[:, p, 2, part], DH),
                                      ALU.mult).then_inc(attn_ready, 1)

            def mask_mix(p):
                for j in range(2):
                    dve.wait_ge(mix_done, 2 * p + j + 1)
                    dve.tensor_tensor(mix[p][:, j * K:(j + 1) * K, :], split(slot(p, j), P), mask.unsqueeze(1).broadcast_to([P, K, P]),
                                      ALU.mult).then_inc(mix_ready, 1)

            def mix_branches(p):
                dve.wait_ge(rest_ready, p + 1)
                for b in range(B2):
                    dve.wait_ge(low_done, 2 * p + b + 1)
                    link(dve.scalar_tensor_tensor(bank(h2[p], b), bank(slot(p, 0), b), weight("proj_b"), coef, ALU.add, ALU.mult))
                    dve.tensor_tensor(x_out[p].rearrange("p (k b n) -> p b k n", k=K, b=B2)[:, b],
                                      bank(h2[p], b).rearrange("p (n k) -> p k n", k=K),
                                      bank(rest[p], b).rearrange("p (n k) -> p k n", k=K), ALU.add).then_inc(xout_ready, 1)

            def residual(p):
                for j in range(2):
                    dve.wait_ge(iw_done, 2 * p + j + 1)
                    dve.tensor_tensor(bank(x1[:, p, :], j), bank(slot(p, 1), j), bank(xs[:, p, :], j), ALU.add).then_inc(x1_ready, 1)

            def norm_tokens(p):
                s = st[:, p]
                for j in range(2):
                    dve.wait_ge(csq_ready, 2 * p + j + 1)
                    (count, link)[j](dve.tensor_reduce(s[:, 0, j * K:(j + 1) * K], split(bank(squares[p], j), H), X, ALU.add))
                count(dve.tensor_scalar(s[:, 2, :], s[:, 0, :], 1.0 / H, LN_EPS, ALU.mult, ALU.add))
                link(dve.tensor_scalar(s[:, 3, :], s[:, 0, :], (1.0 + LN_EPS) / H, LN_EPS ** 2, ALU.mult, ALU.add))
                two = lambda a: s[:, a:a + 2, :].rearrange("p a g -> p (a g)")
                inverse_root(two(4), two(2), two(6))
                for j in range(2):
                    dve.tensor_tensor(split(bank(xc[p], j), H), split(bank(slot(p, 0), j), H), over(s[:, 5, j * K:(j + 1) * K], H),
                                      ALU.mult).then_inc(xn_ready, 1)
                count(dve.tensor_tensor(s[:, 8, :], s[:, 4, :], s[:, 3, :], ALU.mult))
                dve.wait_ge(dve_chain, links[0])
                link(dve.tensor_tensor(s[:, 10, :], s[:, 8, :], s[:, 5, :], ALU.mult))

            def route(p):
                s = st[:, p]
                L = [lg[p][:, n, :, :] for n in range(8)]
                index = const("small_index").unsqueeze(1).broadcast_to([P, G, E])
                dve.wait_ge(router_done, p + 1)
                link(dve.tensor_tensor(L[2], split(slot(p, 0)[:, 0:G * E], E), over(s[:, 10, :], E), ALU.mult))
                link(dve.tensor_tensor(L[0], L[2], weight("br").unsqueeze(1).broadcast_to([P, G, E]), ALU.add))

                def first_at(src, top, picked):
                    link(dve.tensor_tensor(L[6], src, over(top, E), ALU.is_equal))
                    link(dve.tensor_tensor(L[7], L[6], index, ALU.mult))
                    link(dve.tensor_reduce(s[:, 12, :], L[7], X, ALU.max))
                    link(dve.tensor_tensor(picked, L[7], over(s[:, 12, :], E), ALU.is_equal))

                link(dve.tensor_reduce(s[:, 9, :], L[0], X, ALU.max))
                first_at(L[0], s[:, 9, :], L[1])
                link(dve.scalar_tensor_tensor(L[3], L[1], -3e38, L[0], ALU.mult, ALU.add))
                link(dve.tensor_reduce(s[:, 11, :], L[3], X, ALU.max))
                dve.tensor_tensor(s[:, 13, :], s[:, 9, :], s[:, 11, :], ALU.subtract).then_inc(gap_ready, 1)
                first_at(L[3], s[:, 11, :], L[4])

            def shares(p):
                s = st[:, p]
                L = [lg[p][:, n, :, :] for n in range(8)]
                dve.wait_ge(tanh_ready, p + 1)
                count(dve.tensor_scalar(s[:, 15, :], s[:, 14, :], 0.5, 0.5, ALU.mult, ALU.add))
                link(dve.tensor_scalar(s[:, 12, :], s[:, 14, :], -0.5, 0.5, ALU.mult, ALU.add))
                count(dve.tensor_tensor(L[2], L[1], over(s[:, 15, :], E), ALU.mult))
                link(dve.tensor_tensor(L[5], L[4], over(s[:, 12, :], E), ALU.mult))
                link(dve.tensor_tensor(L[6], L[2], L[5], ALU.add))
                link(dve.tensor_copy(gate_parts[:, p, :, 0, :], L[6]))
                dve.tensor_tensor(gate_parts[:, p, :, 1, :], L[6], gate_parts[:, p, :, 0, :], ALU.subtract).then_inc(gparts_ready, 1)

            def biases(p):
                if p == 0:
                    dve.wait_ge(weights_in, 16)
                    dve.wait_ge(bias_t, 1)
                    dve.tensor_tensor(b1p[:, :], slot(0, 0)[:, CHUNK:CHUNK + NT], b1t, ALU.add).then_inc(bias_ready, 1)

            x1f = x1[:, :, :].rearrange("p a n -> p (a n)")

            def finish(i):
                dve.wait_ge(fold_done, i + 1)
                part = x1f[:, bass.ds(i * CHUNK, CHUNK)]
                dve.tensor_tensor(part, g_bank, part, ALU.add).then_inc(res_ready, 1)

            def experts(i, v):
                if v < 0:
                    if not (isinstance(i, int) and i == 0):
                        finish(i - 1)
                    return
                u = UNITS * i + v
                b, m = divmod(v, E // 2)
                dve.wait_ge(w2_done, u + 1)
                dve.wait_ge(gb_ready, u + 1)
                dst = term[:, :] if m else acc[:, b, :]
                if m > 1:
                    dve.wait_ge(add_done, B2 * (E // 2 - 2) * i + (E // 2 - 2) * b + m - 1)
                elif m == 1 and not (isinstance(i, int) and i + b == 0):
                    dve.wait_ge(acc_ready, B2 * i + b)
                dve.scalar_tensor_tensor(dst, y_bank, b2t[:, m:m + 1], gate_b[:, v % 2, :], ALU.add,
                                         ALU.mult).then_inc(term_done, 1)
                if m:
                    dve.wait_ge(term_done, u + 1)
                    total = dve.tensor_tensor(acc[:, b, :], acc[:, b, :], term[:, :], ALU.add)
                    total.then_inc(add_done if m < E // 2 - 1 else acc_ready, 1)

            stages = (norm_columns, first_taps, mask_gram, products, inverse_norms, softmax_in, softmax_out, mask_mix, mix_branches,
                      residual, norm_tokens, route, biases, shares)
            for stage, args in in_turn(stages, experts):
                stage(*args)
            with dve.Fori(STEPS // PAIRS, STEPS) as i:
                for v in range(-1, UNITS):
                    experts(i, v)
            finish(STEPS - 1)


def kernel(**inputs):
    import concourse.bacc as bacc
    from concourse.bass_utils import run_bass_kernel_spmd

    nc = bacc.Bacc("TRN2", target_bir_lowering=False, num_devices=1)
    a = {n: np.asarray(v) for n, v in inputs.items()}
    const32, const16 = constants()
    arrays = {
        "in_x": np.ascontiguousarray(a["x"].transpose(0, 1, 3, 2)),
        "in_small": small_weights(a), "in_W1": a["L0_ffn_W1"], "in_W2": a["L0_ffn_W2"],
        "const32": const32, "const16": const16,
    }
    args = [nc.dram_tensor(n, a.shape, mybir.dt.from_np(a.dtype), kind="ExternalInput").ap() for n, a in arrays.items()]
    out = nc.dram_tensor("block_out", (PAIRS * B2, H, C, W), F32, kind="ExternalOutput").ap()
    metaformer(nc, *args, out)
    r = run_bass_kernel_spmd(nc, [arrays], core_ids=[0])
    return r.results[0]["block_out"].transpose(0, 1, 3, 2)
```
